# Optimizing a Trainium2 kernel written in Bass

```python
import numpy as np
import jax
import jax.numpy as jnp

def _softmax(x, axis=-1):
    return jax.nn.softmax(x, axis=axis)

def _gelu(x):
    return jax.nn.gelu(x, approximate=True)

def _silu(x):
    return jax.nn.silu(x)

def _sigmoid(x):
    return jax.nn.sigmoid(x)

def _layernorm(x, axis=-1, eps=1e-05):
    m = jnp.mean(x, axis=axis, keepdims=True)
    v = jnp.var(x, axis=axis, keepdims=True)
    return (x - m) / jnp.sqrt(v + eps)

def _scatter_add(tgt, idx, src, axis=0):
    return tgt.at[idx].add(src)

def _segment_sum(src, seg, n):
    return jax.ops.segment_sum(src, seg, n)
kernel_name = 'mk_adaln_ffn_d1_seqx_r4_4c2e21'

def setup_inputs(seed: int=0):
    np.random.seed(seed)
    _w = jnp.asarray

    def _rec_inputs():
        import jax
        import jax.numpy as jnp
        _rk = jax.random.key(seed)
        x = 7.971e-05 + 1 * jax.random.normal(jax.random.fold_in(_rk, 1), (8, 512, 256), jnp.float32)
        _lenS = 512 - jax.random.randint(jax.random.fold_in(_rk, 7), (8,), 0, max(1, 512 // 4) + 1, jnp.int32)
        _lenS2 = 512 - jax.random.randint(jax.random.fold_in(_rk, 8), (8,), 0, max(1, 512 // 4) + 1, jnp.int32)
        itok_B_0_6 = jax.random.randint(jax.random.fold_in(_rk, 11), (8,), 0, 7, jnp.int32)
        return (x, itok_B_0_6)
    x, itok_B_0_6 = _rec_inputs()

    def _L0_cond_setup():
        import jax, jax.numpy as jnp
        import numpy as np
        N_PROFILES = 8
        HIDDEN = 256
        BOTTLENECK = 128
        EPS = 1e-05
        key = jax.random.key(seed)
        ks = jax.random.split(key, 8)
        B, S, H, K, P = (16, 512, HIDDEN, BOTTLENECK, N_PROFILES)
        down_w = jax.random.normal(ks[0], (P, H, K), dtype=jnp.float32) * (1.0 / np.sqrt(H))
        down_b = jax.random.normal(ks[1], (P, K), dtype=jnp.float32) * 0.01
        up_w = jax.random.normal(ks[2], (P, K, H), dtype=jnp.float32) * (1.0 / np.sqrt(K))
        up_b = jax.random.normal(ks[3], (P, H), dtype=jnp.float32) * 0.01
        ln_g = jnp.ones((P, H), dtype=jnp.float32)
        ln_b = jnp.zeros((P, H), dtype=jnp.float32)
        hidden = jax.random.normal(ks[4], (B, S, H), dtype=jnp.float32)
        profile_ids = jax.random.randint(ks[5], (B,), 0, P)
        return {'hidden': hidden, 'profile_ids': profile_ids, 'down_w': down_w, 'down_b': down_b, 'up_w': up_w, 'up_b': up_b, 'ln_g': ln_g, 'ln_b': ln_b}
    _L0_cond_all = _L0_cond_setup()
    _L0_cond_in = {k: v for k, v in _L0_cond_all.items() if k in ('down_w', 'down_b', 'up_w', 'up_b', 'ln_g', 'ln_b')}
    del _L0_cond_all

    def _L0_ffn_setup():
        import jax, jax.numpy as jnp
        import numpy as np
        BLOCK = 32
        W_BITS = 4
        ACT_BITS = 16

        def act_qdq(x):
            qmax = 2.0 ** (ACT_BITS - 1) - 1.0
            scale = jnp.maximum(jnp.max(jnp.abs(x)) / qmax, 1e-12)
            return jnp.clip(jnp.round(x / scale), -qmax - 1.0, qmax) * scale

        def fixed_qdq_u16(x):
            scale = 1.0 / 65536.0
            return jnp.clip(jnp.round(x / scale), 0.0, 65535.0) * scale

        def lpbq_dequant(w):
            O, I = w.shape
            qmax = 2.0 ** (W_BITS - 1) - 1.0
            wb = w.reshape(O, I // BLOCK, BLOCK)
            s = jnp.maximum(jnp.max(jnp.abs(wb), axis=-1, keepdims=True) / qmax, 1e-12)
            wq = jnp.clip(jnp.round(wb / s), -qmax - 1.0, qmax) * s
            return wq.reshape(O, I)
        key = jax.random.key(seed)
        k1, k2, k3, k4 = jax.random.split(key, 4)
        B, S, H, I = (2, 1024, 256, 768)
        x = jax.random.normal(k1, (B, S, H), jnp.float32)
        w_gate = jax.random.normal(k2, (I, H), jnp.float32) * 0.02
        w_up = jax.random.normal(k3, (I, H), jnp.float32) * 0.02
        w_down = jax.random.normal(k4, (H, I), jnp.float32) * 0.02
        return {'x': x, 'w_gate': w_gate, 'w_up': w_up, 'w_down': w_down}
    _L0_ffn_all = _L0_ffn_setup()
    _L0_ffn_in = {k: v for k, v in _L0_ffn_all.items() if k in ('w_gate', 'w_up', 'w_down')}
    del _L0_ffn_all
    return {'x': x, 'itok_B_0_6': itok_B_0_6, 'L0_cond_down_w': _L0_cond_in['down_w'], 'L0_cond_down_b': _L0_cond_in['down_b'], 'L0_cond_up_w': _L0_cond_in['up_w'], 'L0_cond_up_b': _L0_cond_in['up_b'], 'L0_cond_ln_g': _L0_cond_in['ln_g'], 'L0_cond_ln_b': _L0_cond_in['ln_b'], 'L0_ffn_w_gate': _L0_ffn_in['w_gate'], 'L0_ffn_w_up': _L0_ffn_in['w_up'], 'L0_ffn_w_down': _L0_ffn_in['w_down']}

def reference(x, itok_B_0_6, L0_cond_down_w, L0_cond_down_b, L0_cond_up_w, L0_cond_up_b, L0_cond_ln_g, L0_cond_ln_b, L0_ffn_w_gate, L0_ffn_w_up, L0_ffn_w_down):
    import jax
    import jax.numpy as jnp

    def _L0_cond_ref(hidden, profile_ids, down_w, down_b, up_w, up_b, ln_g, ln_b):
        import jax, jax.numpy as jnp
        import numpy as np
        N_PROFILES = 8
        HIDDEN = 256
        BOTTLENECK = 128
        EPS = 1e-05
        Wd = down_w[profile_ids]
        bd = down_b[profile_ids][:, None]
        Wu = up_w[profile_ids]
        bu = up_b[profile_ids][:, None]
        g = ln_g[profile_ids][:, None]
        b = ln_b[profile_ids][:, None]
        z = jax.nn.relu(jnp.einsum('bsh,bhk->bsk', hidden, Wd) + bd)
        y = hidden + jnp.einsum('bsk,bkh->bsh', z, Wu) + bu
        mu = jnp.mean(y, axis=-1, keepdims=True)
        var = jnp.mean(jnp.square(y - mu), axis=-1, keepdims=True)
        return (y - mu) * jax.lax.rsqrt(var + EPS) * g + b

    def _L0_ffn_ref(x, w_gate, w_up, w_down):
        import jax, jax.numpy as jnp
        import numpy as np
        BLOCK = 32
        W_BITS = 4
        ACT_BITS = 16

        def act_qdq(x):
            qmax = 2.0 ** (ACT_BITS - 1) - 1.0
            scale = jnp.maximum(jnp.max(jnp.abs(x)) / qmax, 1e-12)
            return jnp.clip(jnp.round(x / scale), -qmax - 1.0, qmax) * scale

        def fixed_qdq_u16(x):
            scale = 1.0 / 65536.0
            return jnp.clip(jnp.round(x / scale), 0.0, 65535.0) * scale

        def lpbq_dequant(w):
            O, I = w.shape
            qmax = 2.0 ** (W_BITS - 1) - 1.0
            wb = w.reshape(O, I // BLOCK, BLOCK)
            s = jnp.maximum(jnp.max(jnp.abs(wb), axis=-1, keepdims=True) / qmax, 1e-12)
            wq = jnp.clip(jnp.round(wb / s), -qmax - 1.0, qmax) * s
            return wq.reshape(O, I)
        x = act_qdq(x)
        up = act_qdq(x @ lpbq_dequant(w_up).T)
        gate = act_qdq(x @ lpbq_dequant(w_gate).T)
        sig = fixed_qdq_u16(jax.nn.sigmoid(gate))
        gate = act_qdq(gate * sig)
        o = act_qdq(gate * up)
        return o @ lpbq_dequant(w_down).T
    x = x + _L0_ffn_ref(_L0_cond_ref(x, itok_B_0_6, L0_cond_down_w, L0_cond_down_b, L0_cond_up_w, L0_cond_up_b, L0_cond_ln_g, L0_cond_ln_b), L0_ffn_w_gate, L0_ffn_w_up, L0_ffn_w_down)
    return x

_drawn_inputs = setup_inputs


def setup_inputs(seed=0):
    import zlib

    import numpy as np

    out = dict(_drawn_inputs(seed))
    spreads = {'L0_cond_ln_g': (1.0, 0.6), 'L0_cond_ln_b': (0.0, 0.8)}
    factors = {'L0_cond_down_b': 64.0, 'L0_cond_up_b': 64.0}
    for name, (base, spread) in spreads.items():
        noise = np.random.default_rng([zlib.crc32(name.encode()), seed]).standard_normal(out[name].shape)
        drawn = base * np.exp(spread * noise) if base else spread * noise
        out[name] = jnp.asarray(drawn.astype(out[name].dtype))
    for name, factor in factors.items():
        out[name] = (out[name] * factor).astype(out[name].dtype)
    return out
```

```python
from contextlib import ExitStack

import concourse.bass as bass
from concourse import mybir

P = 128
F32 = mybir.dt.float32
I16 = mybir.dt.int16
I32 = mybir.dt.int32
ALU = mybir.AluOpType
ACT = mybir.ActivationFunctionType
AX = mybir.AxisListType

BLOCK = 32
W_QMAX = 7.0
A_QMAX = 32767.0
TINY = 1e-12
LN_EPS = 1e-5
SIG_STEPS = 65536.0
INT_ROUND = 1.5 * 2.0 ** 23


def adaln_ffn_kernel(nc, x, profile, down_w, down_b, up_w, up_b, ln_g, ln_b, w_gate, w_up, w_down, out):
    T, S, H = x.shape
    NPROF, _, K = down_w.shape
    I = w_gate.shape[0]
    Q = S // P
    HC, IC = H // P, I // P
    NPAIR = IC // 2
    TE = HC * S
    TI = IC * S
    HALF = TI // 2
    WN = HC * I
    KEEP = T // 2
    assert S == 512 and K == P and IC % 2 == 0 and T % 4 == 0 and Q % 2 == 0

    x_t = x.rearrange("t (p q) h -> t p (q h)", q=Q)
    out_t = out.rearrange("t (p q) h -> t p (q h)", q=Q)
    spill = nc.dram_tensor("up_spill", [KEEP, P, TI], F32, kind="Internal").ap()

    with ExitStack() as ctx:
        def sb(name, shape, dt=F32):
            return ctx.enter_context(nc.sbuf_tensor(name, shape, dt))

        def sem(name):
            return ctx.enter_context(nc.semaphore(name))

        gbuf = sb("gbuf", [P, HALF + T * TI])
        CQ = T * TE
        UQ0 = CQ - HALF
        ubuf = sb("ubuf", [P, CQ + KEEP * TI])
        wgT = sb("wgT", [P, WN])
        wuT = sb("wuT", [P, WN])
        wdT = sb("wdT", [P, WN])
        gint = sb("gint", [P, 2, HALF], I16)
        NPC = 1 + 2 * HC
        pcols = sb("pcols", [P, NPC, T])
        ids = sb("ids", [NPROF, T], I32)
        hot = sb("hot", [NPROF, T])
        prof_i = sb("prof_i", [NPROF, 1], I32)
        prof = sb("prof", [NPROF, 1])
        sc = sb("sc", [P, 32])
        mx = sb("mx", [P, 3 * T])
        mx2 = sb("mx2", [P, 2 * T])
        pm = sb("pm", [P, 2])
        row = sb("row", [1, 2])
        ones = sb("ones", [1, P])
        ident = sb("ident", [P, P])
        ps = ctx.enter_context(nc.psum_tensor("ps", [P, 8, 512], F32))

        hq16 = gbuf[:, 0:T * HALF].bitcast(I16)
        uq16 = ubuf[:, UQ0:UQ0 + T * HALF].bitcast(I16)

        def gtile(t, half=None):
            o = HALF + TI * t
            return gbuf[:, bass.ds(o, TI)] if half is None else gbuf[:, bass.ds(o + HALF * half, HALF)]

        def uslot(s):
            return ubuf[:, bass.ds(CQ + TI * s, TI)]

        at = [0]

        def cut(buf, n):
            at[0] += n
            return buf[:, at[0] - n:at[0]]

        xs = [cut(gbuf, TE) for _ in range(T)]
        wd = [cut(gbuf, HC * K) for _ in range(T)]
        wu = [cut(gbuf, H) for _ in range(T)]
        bu = [cut(gbuf, H) for _ in range(T)]
        xT = [cut(gbuf, TE) for _ in range(2)]
        xb = [cut(gbuf, TE) for _ in range(2)]
        ys = [cut(gbuf, TE) for _ in range(2)]
        yn = [cut(gbuf, TE) for _ in range(2)]
        zT = [cut(gbuf, S) for _ in range(2)]
        prows = cut(gbuf, K + 2 * H)[0:NPROF, :]
        NB = WN // BLOCK
        wscale = cut(gbuf, 3 * 2 * NB).rearrange("p (m k n) -> p m k n", m=3, k=2)
        stats = cut(gbuf, 2 * Q * 6).rearrange("p (s q n) -> p s q n", s=2, q=Q)
        assert at[0] <= HALF + T * TI
        mv = sb("mv", [P, 2, Q, 2])
        rstd = sb("rstd", [P, 2, Q])
        half_neg = sb("half_neg", [P, Q])
        at[0] = CQ
        wnat = [cut(ubuf, WN) for _ in range(3)]
        wdeq = [cut(ubuf, WN) for _ in range(3)]
        assert at[0] <= CQ + KEEP * TI

        base = HALF + KEEP * TI
        oq32 = [gbuf[:, base + TI * s:base + TI * (s + 1)] for s in range(2)]
        oq16 = [gbuf[:, base + 2 * TI + HALF * s:base + 2 * TI + HALF * (s + 1)].bitcast(I16) for s in range(2)]
        xr = [gbuf[:, base + 3 * TI + TE * s:base + 3 * TI + TE * (s + 1)] for s in range(2)]
        ot = [ubuf[:, TE * s:TE * (s + 1)] for s in range(2)]
        prod = [wgT[:, :], wuT[:, :]]
        assert HALF == WN

        ids_in, prow_in = sem("ids_in"), sem("prow_in")
        x_in = [sem(f"x_in{t}") for t in range(T)]
        w_in = [sem(f"w_in{t}") for t in range(T)]
        wnat_in = [sem(f"wnat_in{m}") for m in range(3)]
        const_ok, hot_ok = sem("const_ok"), sem("hot_ok")
        pcol_ps, pcol_sb = sem("pcol_ps"), sem("pcol_sb")
        xT_ps, xT_sb, z_ps, z_sb, y_ps, y_sb = (sem(n) for n in ("xT_ps", "xT_sb", "z_ps", "z_sb", "y_ps", "y_sb"))
        xb_ok, stat_ok, mv_ok, var_ok, rstd_ok, yn_ok = (sem(n) for n in ("xb_ok", "stat_ok", "mv_ok", "var_ok", "rstd_ok", "yn_ok"))
        c_ps, c_sb, cmax_ok = sem("c_ps"), sem("c_sb"), sem("cmax_ok")
        wamax_ok, wscale_ok, wint_ok, wdeq_ok, wT_ps, wT_sb = (
            sem(n) for n in ("wamax_ok", "wscale_ok", "wint_ok", "wdeq_ok", "wT_ps", "wT_sb"))
        max_ok, maxT_ps, max_row, max_bc = (sem(n) for n in ("max_ok", "maxT_ps", "max_row", "max_bc"))
        calc = sem("calc")
        cround, cq_ok = sem("cround"), sem("cq_ok")
        pair_ps = sem("pair_ps")
        pair_sb = sem("pair_sb")
        gmax_ok, umax_ok, hmax_ok = sem("gmax_ok"), sem("umax_ok"), sem("hmax_ok")
        kg_ok, khu_ok, ko_ok = sem("kg_ok"), sem("khu_ok"), sem("ko_ok")
        gint_ok, sig_ok, sigq_ok, h_ok = (sem(n) for n in ("gint_ok", "sig_ok", "sigq_ok", "h_ok"))
        spilled = sem("spilled")
        reload = [sem(f"reload{i}") for i in range(T - KEEP)]
        hq_ok, uq_ok, prod_ok, omax_ok = (sem(n) for n in ("hq_ok", "uq_ok", "prod_ok", "omax_ok"))
        oq16_ok, oq32_ok, o_ps, o_sb = (sem(n) for n in ("oq16_ok", "oq32_ok", "o_ps", "o_sb"))
        xr_in = [sem(f"xr_in{s}") for s in range(2)]
        stored = [sem(f"stored{s}") for s in range(2)]

        turns = [[(1, wuT, 0, 8, 6)], [(1, wuT, 8, 12, 6), (2, wdT, 0, 4, 7)], [(2, wdT, 4, 12, 6)]]
        NTURN = len(turns)
        assert IC * HC == 12
        S_C, INV_C, S_G, K_G, S_U, K_U, S_H, K_H, S_HU, S_O, K_O, S_GS, TMP = range(13)

        def col(k):
            return sc[:, k:k + 1]

        ctx.enter_context(nc.allow_non_contiguous_dma(reason="rows of biases"))
        block = ctx.enter_context(nc.Block())

        @block.sync
        def _(sp):
            sp.dma_start(ids[:, :], profile.rearrange("(a t) -> a t", a=1).to_broadcast([NPROF, T])).then_inc(ids_in, 16)
            sp.dma_start(xs[0], x_t[0]).then_inc(x_in[0], 16)
            sp.dma_start(prows[:, 0:K], down_b).then_inc(prow_in, 16)
            sp.dma_start(prows[:, K:K + H], ln_g).then_inc(prow_in, 16)
            sp.dma_start(prows[:, K + H:K + 2 * H], ln_b).then_inc(prow_in, 16)
            sp.wait_ge(ids_in, 16)
            for t in range(T):
                r = sp.value_load(ids[0:1, t:t + 1], min_val=0, max_val=NPROF - 1)
                sp.dma_start(wd[t].rearrange("p (c k) -> p c k", c=HC),
                             down_w[bass.ds(r, 1), :, :].rearrange("a (c p) k -> p (a c) k", p=P)).then_inc(w_in[t], 16)
                sp.dma_start(wu[t], up_w[bass.ds(r, 1), :, :].rearrange("a k h -> k (a h)")).then_inc(w_in[t], 16)
                sp.dma_start(bu[t], up_b[bass.ds(r, 1), :].to_broadcast([P, H])).then_inc(w_in[t], 16)
                if t + 1 < T:
                    sp.dma_start(xs[t + 1], x_t[t + 1]).then_inc(x_in[t + 1], 16)
                for m, (after, w) in enumerate(((2, w_gate), (T - 2, w_up), (T - 1, w_down))):
                    if t == after:
                        sp.dma_start(wnat[m].rearrange("p (c k) -> p c k", k=w.shape[1]),
                                     w.rearrange("(c p) k -> p c k", p=P)).then_inc(wnat_in[m], 16)
            for n in range(KEEP):
                sp.wait_ge(pair_sb, 3 + NPAIR * (T + 1 + n))
                sp.dma_start(spill[n], uslot(n)).then_inc(spilled, 16)
                sp.wait_ge(spilled, 16 * n + 16)
            sp.wait_ge(pair_ps, 2 * T * NPAIR)
            sp.dma_start(ubuf[:, 0:TI], spill[0]).then_inc(reload[0], 16)
            sp.dma_start(ubuf[:, TI:2 * TI], spill[1]).then_inc(reload[1], 16)
            sp.wait_ge(uq_ok, KEEP)
            sp.dma_start(uslot(KEEP - 1), spill[2]).then_inc(reload[2], 16)
            sp.wait_ge(hq_ok, KEEP + 1)
            sp.dma_start(gtile(KEEP), spill[3]).then_inc(reload[3], 16)
            sp.wait_ge(hq_ok, T)
            for s in range(2):
                sp.dma_start(xr[s], x_t[s]).then_inc(xr_in[s], 16)
            with sp.Fori(0, T // 2 - 1) as k:
                for s in range(2):
                    sp.wait_ge(o_sb, 2 * k + s + 1)
                    sp.wait_ge(hq_ok, T)
                    sp.dma_start(out_t[bass.ds(2 * k + s, 1)].rearrange("a p n -> p (a n)"), ot[s]).then_inc(stored[s], 16)
                    sp.dma_start(xr[s], x_t[bass.ds(2 * k + 2 + s, 1)].rearrange("a p n -> p (a n)")).then_inc(xr_in[s], 16)
            for s in range(2):
                sp.wait_ge(o_sb, T - 2 + s + 1)
                sp.dma_start(out_t[T - 2 + s], ot[s]).then_inc(stored[s], 16)
            for s in range(2):
                sp.wait_ge(stored[s], 16 * (T // 2))

        @block.gpsimd
        def _(pool):
            pool.memset(ident[:, :], 0.0).then_inc(const_ok, 1)
            pool.wait_ge(const_ok, 1)
            pool.affine_select(out=ident[:, :], in_=ident[:, :], compare_op=ALU.not_equal, fill=1.0, base=0,
                               pattern=[[-1, P]], channel_multiplier=1).then_inc(const_ok, 1)
            pool.memset(ones[:, :], 1.0).then_inc(const_ok, 1)
            pool.memset(half_neg[:, :], -0.5).then_inc(const_ok, 1)
            pool.iota(prof_i[:, :], pattern=[[0, 1]], base=0, channel_multiplier=1).then_inc(const_ok, 1)

            def add_bias(t):
                pool.wait_ge(x_in[t], 16)
                pool.wait_ge(w_in[t], 48)
                if t >= 2:
                    pool.wait_ge(y_sb, t - 1)
                pool.tensor_tensor(xb[t % 2].rearrange("p (q h) -> p q h", q=Q),
                                   xs[t].rearrange("p (q h) -> p q h", q=Q),
                                   bu[t].rearrange("p (a h) -> p a h", a=1).to_broadcast([P, Q, H]),
                                   ALU.add).then_inc(xb_ok, 1)

            def quantise_weight(m):
                pool.wait_ge(wscale_ok, m + 1)
                wide, fine = (v.rearrange("p (n b) -> p n b", b=BLOCK) for v in (wnat[m], wdeq[m]))
                s, inv = (wscale[:, m, k, :].rearrange("p (n a) -> p n a", a=1).to_broadcast([P, NB, BLOCK]) for k in (0, 1))
                pool.tensor_tensor(fine, wide, inv, ALU.mult).then_inc(wint_ok, 1)
                pool.wait_ge(wint_ok, 3 * m + 1)
                pool.tensor_scalar(wdeq[m], wdeq[m], 1.0, INT_ROUND, ALU.mult, ALU.add).then_inc(wint_ok, 1)
                pool.wait_ge(wint_ok, 3 * m + 2)
                pool.tensor_scalar(wdeq[m], wdeq[m], -INT_ROUND, 1.0, ALU.add, ALU.mult).then_inc(wint_ok, 1)
                pool.wait_ge(wint_ok, 3 * m + 3)
                pool.tensor_tensor(fine, fine, s, ALU.mult).then_inc(wdeq_ok, 1)

            add_bias(0)
            add_bias(1)
            for t in range(T):
                pool.wait_ge(var_ok, t + 1)
                pool.tensor_tensor(rstd[:, t % 2, :], rstd[:, t % 2, :], half_neg[:, :], ALU.pow).then_inc(rstd_ok, 1)
                if t + 2 < T:
                    add_bias(t + 2)
                if t == 4:
                    quantise_weight(0)
            quantise_weight(1)
            quantise_weight(2)

            for n in range(2 * T):
                pool.wait_ge(sig_ok, n + 1)
                g = gtile(n // 2, n % 2)
                pool.tensor_scalar(g.bitcast(I32), g, SIG_STEPS, 0.0, ALU.mult, ALU.add).then_inc(sigq_ok, 1)

            pool.wait_ge(khu_ok, 1)
            for t in range(T):
                if t:
                    pool.wait_ge(hq_ok, t)
                pool.tensor_scalar(hq16[:, TI * t:TI * (t + 1)], gtile(t), col(K_H), 1.0, ALU.mult, ALU.mult)\
                    .then_inc(hq_ok, 1)

        @block.scalar
        def _(act):
            def copy_xT(t):
                act.wait_ge(xT_ps, t + 1)
                if t >= 2:
                    act.wait_ge(z_ps, t - 1)
                act.activation(xT[t % 2], ps[:, 0:HC, :], ACT.Copy).then_inc(xT_sb, 1)

            def relu_z(t):
                act.wait_ge(z_ps, t + 1)
                if t >= 2:
                    act.wait_ge(y_ps, t - 1)
                act.activation(zT[t % 2], ps[:, 2, :], ACT.Relu, bias=pcols[:, 0, t:t + 1]).then_inc(z_sb, 1)

            def scale_c(t):
                act.wait_ge(c_ps, t + 1)
                for c in range(HC):
                    act.activation(ubuf[:, TE * t + S * c:TE * t + S * (c + 1)], ps[:, 5 + c, :], ACT.Identity,
                                   scale=pcols[:, 1 + c, t:t + 1], bias=pcols[:, 1 + HC + c, t:t + 1]).then_inc(c_sb, 1)

            copy_xT(0)
            act.wait_ge(pcol_ps, 1)
            act.activation(pcols[:, :, :], ps[:, 7, 0:NPC * T].rearrange("p (n t) -> p n t", t=T), ACT.Copy).then_inc(pcol_sb, 1)
            act.wait_ge(pcol_sb, 1)

            for t in range(T):
                if t + 1 < T:
                    copy_xT(t + 1)
                relu_z(t)
                if t >= 2:
                    scale_c(t - 2)
            for t in range(T - 2, T):
                scale_c(t)

            def copy_weights(r):
                act.wait_ge(wT_ps, r + 2)
                for _, wT, lo, hi, bank in turns[r]:
                    banks = (hi - lo) // 4
                    act.activation(wT[:, P * lo:P * hi], ps[:, bank:bank + banks, :].rearrange("p b n -> p (b n)"),
                                   ACT.Copy).then_inc(wT_sb, 1)

            def copy_gate(t):
                for q in range(NPAIR):
                    act.wait_ge(pair_ps, NPAIR * t + q + 1)
                    act.wait_ge(max_bc, 1)
                    act.activation(gbuf[:, bass.ds(HALF + TI * t + 2 * S * q, 2 * S)], ps[:, 2 * q:2 * q + 2, :],
                                   ACT.Copy).then_inc(pair_sb, 1)

            act.wait_ge(wT_ps, 1)
            for b in range(NPAIR):
                act.activation(wgT[:, 4 * P * b:4 * P * (b + 1)], ps[:, b, :], ACT.Copy).then_inc(pair_sb, 1)
            with act.Fori(0, T - NTURN) as t:
                copy_gate(t)
            for r in range(NTURN):
                copy_weights(r)
                copy_gate(T - NTURN + r)

            act.wait_ge(kg_ok, 1)
            for part in range(2):
                with act.Fori(0, KEEP) as n:
                    k = n + part * KEEP

                    def copy_up(q):
                        act.wait_ge(pair_ps, NPAIR * (T + k) + q + 1)
                        act.wait_ge(kg_ok, 1)
                        act.activation(ubuf[:, bass.ds(CQ + TI * n + 2 * S * q, 2 * S)], ps[:, 2 * q:2 * q + 2, :],
                                       ACT.Copy).then_inc(pair_sb, 1)

                    for h in range(2):
                        act.wait_ge(h_ok, 2 * k + h + 1)
                        act.activation(gint[:, h, :], gtile(k, h), ACT.Copy, scale=col(K_G)).then_inc(gint_ok, 1)
                        if part and not h:
                            act.wait_ge(spilled, 16 * n + 16)
                            act.wait_ge(umax_ok, NPAIR * (n + 1))
                        act.wait_ge(gint_ok, 2 * k + h + 1)
                        copy_up(h)
                        act.activation(gtile(k, h), gint[:, h, :], ACT.Sigmoid, scale=col(S_G)).then_inc(sig_ok, 1)
                    copy_up(2)

            act.wait_ge(khu_ok, 1)
            with act.Fori(0, KEEP) as t:
                act.activation(uq16[:, bass.ds(TI * t, TI)], uslot(t), ACT.Copy, scale=col(K_U)).then_inc(uq_ok, 1)
                act.wait_ge(uq_ok, t + 1)
            for i, src in enumerate((ubuf[:, 0:TI], ubuf[:, TI:2 * TI], uslot(KEEP - 1), gtile(KEEP))):
                act.wait_ge(reload[i], 16)
                act.wait_ge(uq_ok, KEEP + i)
                act.activation(uq16[:, TI * (KEEP + i):TI * (KEEP + i + 1)], src, ACT.Copy, scale=col(K_U)).then_inc(uq_ok, 1)

            def widen(k, s):
                for h in range(2):
                    act.wait_ge(oq16_ok, 4 * k + 2 * s + h + 1)
                    act.activation(oq32[s][:, HALF * h:HALF * (h + 1)], oq16[s][:, HALF * h:HALF * (h + 1)],
                                   ACT.Copy).then_inc(oq32_ok, 1)

            for s in range(2):
                widen(0, s)
            with act.Fori(1, T // 2) as k:
                for s in range(2):
                    act.wait_ge(o_ps, 2 * k + s - 1)
                    widen(k, s)

        @block.vector
        def _(dve):
            count = [0]

            def small(ins):
                count[0] += 1
                ins.then_inc(calc, 1)
                dve.wait_ge(calc, count[0])

            def reduce_abs(o, i):
                return dve.tensor_reduce(o, i, AX.X, ALU.max, apply_absolute_value=True)

            rounds = [0]

            def global_max(sources):
                rounds[0] += 1
                for k, s in enumerate(sources):
                    small(dve.reduce_max(pm[:, k:k + 1], s, AX.X))
                dve.sem_inc(max_ok, 1)
                dve.wait_ge(maxT_ps, rounds[0])
                n = len(sources)
                dve.tensor_reduce(row[:, 0:n], ps[0:1, 7, 0:n * P].rearrange("a (n p) -> a n p", p=P), AX.X,
                                  ALU.max).then_inc(max_row, 1)
                dve.wait_ge(max_bc, rounds[0])
                return [ps[:, 7, 256 + k:257 + k] for k in range(n)]

            dve.wait_ge(const_ok, 5)
            dve.wait_ge(ids_in, 16)
            small(dve.tensor_copy(prof[:, :], prof_i[:, :]))
            dve.tensor_scalar(hot[:, :], ids[:, :], prof[:, 0:1], None, ALU.is_equal).then_inc(hot_ok, 1)

            def weight_scales(m):
                dve.wait_ge(wnat_in[m], 16)
                reduce_abs(wscale[:, m, 1, :], wnat[m].rearrange("p (n b) -> p n b", b=BLOCK)).then_inc(wamax_ok, 1)
                dve.wait_ge(wamax_ok, m + 1)
                small(dve.tensor_scalar(wscale[:, m, 0, :], wscale[:, m, 1, :], 1.0 / W_QMAX, TINY, ALU.mult, ALU.max))
                dve.reciprocal(wscale[:, m, 1, :], wscale[:, m, 0, :]).then_inc(wscale_ok, 1)

            def take_cmax(t):
                dve.wait_ge(c_sb, HC * (t + 1))
                reduce_abs(mx[:, t:t + 1], ubuf[:, TE * t:TE * (t + 1)]).then_inc(cmax_ok, 1)

            for t in range(T):
                s = t % 2
                if t == 4:
                    weight_scales(0)
                dve.wait_ge(y_ps, t + 1)
                dve.wait_ge(xb_ok, t + 1)
                dve.tensor_tensor(ys[s], ps[:, 3:5, :].rearrange("p a n -> p (a n)"), xb[s], ALU.add).then_inc(y_sb, 1)
                dve.wait_ge(y_sb, t + 1)
                for q in range(Q):
                    dve.bn_stats(stats[:, s, q, :], ys[s][:, H * q:H * (q + 1)]).then_inc(stat_ok, 1)
                for q in range(Q):
                    dve.wait_ge(stat_ok, Q * t + q + 1)
                    ins = dve.bn_aggr(mv[:, s, q, :], stats[:, s, q, :])
                ins.then_inc(mv_ok, 1)
                dve.wait_ge(mv_ok, t + 1)
                dve.tensor_scalar(rstd[:, s, :], mv[:, s, :, 1], LN_EPS, None, ALU.add).then_inc(var_ok, 1)
                if t >= 2:
                    take_cmax(t - 2)
                dve.wait_ge(rstd_ok, t + 1)
                if t >= 2:
                    dve.wait_ge(c_ps, t - 1)
                for q in range(Q):
                    ins = dve.tensor_scalar(yn[s][:, H * q:H * (q + 1)], ys[s][:, H * q:H * (q + 1)],
                                            mv[:, s, q, 0:1], rstd[:, s, q:q + 1], ALU.subtract, ALU.mult)
                ins.then_inc(yn_ok, 1)
            for t in range(T - 2, T):
                take_cmax(t)

            dve.wait_ge(cmax_ok, T)
            cmax, = global_max([mx[:, 0:T]])
            small(dve.tensor_scalar(col(S_C), cmax, 1.0 / A_QMAX, TINY, ALU.mult, ALU.max))
            small(dve.reciprocal(col(INV_C), col(S_C)))
            with dve.Fori(0, T) as t:
                ct = ubuf[:, bass.ds(TE * t, TE)]
                dve.tensor_scalar(ct, ct, col(INV_C), INT_ROUND, ALU.mult, ALU.add).then_inc(cround, 1)
                dve.wait_ge(cround, t + 1)
                dve.tensor_scalar(ct, ct, INT_ROUND, None, ALU.subtract).then_inc(cq_ok, 1)
            for m in (1, 2):
                weight_scales(m)
            with dve.Fori(0, T) as t:
                for q in range(NPAIR):
                    dve.wait_ge(pair_sb, 3 + NPAIR * t + q + 1)
                    reduce_abs(mx[:, bass.ds(NPAIR * t + q, 1)],
                               gbuf[:, bass.ds(HALF + TI * t + 2 * S * q, 2 * S)]).then_inc(gmax_ok, 1)
            dve.wait_ge(gmax_ok, NPAIR * T)
            gmax, = global_max([mx[:, 0:NPAIR * T]])
            small(dve.tensor_scalar(col(TMP), gmax, col(S_C), 1.0 / A_QMAX, ALU.mult, ALU.mult))
            small(dve.tensor_scalar(col(S_G), col(TMP), TINY, None, ALU.max))
            small(dve.reciprocal(col(TMP), col(S_G)))
            dve.tensor_scalar(col(K_G), col(TMP), col(S_C), None, ALU.mult).then_inc(kg_ok, 1)

            dve.sem_inc(h_ok, 2)
            for part in range(2):
                with dve.Fori(0, KEEP) as n:
                    k = n + part * KEEP
                    for h in range(2):
                        g = gtile(k, h)
                        dve.wait_ge(sigq_ok, 2 * k + h + 1)
                        dve.scalar_tensor_tensor(g, g.bitcast(I32), SIG_STEPS - 1.0, gint[:, h, :], ALU.min, ALU.mult)\
                           .then_inc(h_ok, 1)
                        dve.wait_ge(h_ok, 2 * k + h + 3)
                        reduce_abs(mx2[:, bass.ds(2 * k + h, 1)], g).then_inc(hmax_ok, 1)
                    for q in range(NPAIR):
                        dve.wait_ge(pair_sb, 3 + NPAIR * (T + k) + q + 1)
                        reduce_abs(mx[:, bass.ds(NPAIR * k + q, 1)],
                                   ubuf[:, bass.ds(CQ + TI * n + 2 * S * q, 2 * S)]).then_inc(umax_ok, 1)
            dve.wait_ge(hmax_ok, 2 * T)
            dve.wait_ge(umax_ok, NPAIR * T)
            hmax, umax = global_max([mx2[:, 0:2 * T], mx[:, 0:NPAIR * T]])
            small(dve.tensor_scalar(col(S_GS), col(S_G), 1.0 / SIG_STEPS, None, ALU.mult))
            for mxp, unit, s_, k_ in ((hmax, S_GS, S_H, K_H), (umax, S_C, S_U, K_U)):
                small(dve.tensor_scalar(col(TMP), mxp, col(unit), 1.0 / A_QMAX, ALU.mult, ALU.mult))
                small(dve.tensor_scalar(col(s_), col(TMP), TINY, None, ALU.max))
                small(dve.reciprocal(col(TMP), col(s_)))
                small(dve.tensor_scalar(col(k_), col(TMP), col(unit), None, ALU.mult))
            dve.sem_inc(khu_ok, 1)

            with dve.Fori(0, T) as t:
                dve.wait_ge(hq_ok, t + 1)
                dve.wait_ge(uq_ok, t + 1)
                for h in range(2):
                    o = TI * t + HALF * h
                    dve.tensor_tensor(prod[h], hq16[:, bass.ds(o, HALF)], uq16[:, bass.ds(o, HALF)], ALU.mult)\
                       .then_inc(prod_ok, 1)
                    dve.wait_ge(prod_ok, 2 * t + h + 1)
                    reduce_abs(mx[:, bass.ds(2 * t + h, 1)], prod[h]).then_inc(omax_ok, 1)
            dve.wait_ge(omax_ok, 2 * T)
            omax, = global_max([mx[:, 0:2 * T]])
            small(dve.tensor_scalar(col(S_HU), col(S_H), col(S_U), None, ALU.mult))
            small(dve.tensor_scalar(col(TMP), omax, col(S_HU), 1.0 / A_QMAX, ALU.mult, ALU.mult))
            small(dve.tensor_scalar(col(S_O), col(TMP), TINY, None, ALU.max))
            small(dve.reciprocal(col(TMP), col(S_O)))
            small(dve.tensor_scalar(col(K_O), col(TMP), col(S_HU), None, ALU.mult))

            def round_product(t, s):
                for h in range(2):
                    o = TI * t + HALF * h
                    dve.scalar_tensor_tensor(oq16[s][:, HALF * h:HALF * (h + 1)], hq16[:, bass.ds(o, HALF)], col(K_O),
                                             uq16[:, bass.ds(o, HALF)], ALU.mult, ALU.mult).then_inc(oq16_ok, 1)

            def add_residual(k, s, wait_stored=True):
                t = 2 * k + s
                dve.wait_ge(o_ps, t + 1)
                dve.wait_ge(xr_in[s], 16 * k + 16)
                if wait_stored:
                    dve.wait_ge(stored[s], 16 * k)
                dve.scalar_tensor_tensor(ot[s], ps[:, 2 * s:2 * s + 2, :].rearrange("p a n -> p (a n)"), col(S_O),
                                         xr[s], ALU.mult, ALU.add).then_inc(o_sb, 1)

            for s in range(2):
                round_product(s, s)
            for s in range(2):
                dve.wait_ge(oq32_ok, 2 * s + 2)
                round_product(2 + s, s)
                add_residual(0, s, wait_stored=False)
            with dve.Fori(1, T // 2 - 1) as k:
                for s in range(2):
                    dve.wait_ge(oq32_ok, 4 * k + 2 * s + 2)
                    round_product(2 * k + 2 + s, s)
                    add_residual(k, s)
            for s in range(2):
                add_residual(T // 2 - 1, s)

        @block.tensor
        def _(pe):
            pe.wait_ge(const_ok, 5)
            def transpose_x(t):
                pe.wait_ge(x_in[t], 16)
                if t >= 1:
                    pe.wait_ge(xT_sb, t)
                for c in range(HC):
                    for q in range(Q):
                        ins = pe.transpose(ps[:, c, P * q:P * (q + 1)], xs[t][:, H * q + P * c:H * q + P * (c + 1)], ident[:, :])
                ins.then_inc(xT_ps, 1)

            def project_down(t):
                pe.wait_ge(w_in[t], 48)
                pe.wait_ge(xT_sb, t + 1)
                if t >= 1:
                    pe.wait_ge(z_sb, t)
                for c in range(HC):
                    ins = pe.matmul(ps[:, 2, :], wd[t][:, K * c:K * (c + 1)], xT[t % 2][:, S * c:S * (c + 1)],
                                    start=c == 0, stop=c == HC - 1)
                ins.then_inc(z_ps, 1)

            def project_up(t):
                pe.wait_ge(z_sb, t + 1)
                if t >= 1:
                    pe.wait_ge(y_sb, t)
                for q in range(Q):
                    ins = pe.matmul(ps[:, 3 + q // 2, H * (q % 2):H * (q % 2 + 1)], zT[t % 2][:, P * q:P * (q + 1)],
                                    wu[t], start=True, stop=True)
                ins.then_inc(y_ps, 1)

            def transpose_y(t):
                pe.wait_ge(yn_ok, t + 1)
                if t >= 1:
                    pe.wait_ge(c_sb, HC * t)
                for c in range(HC):
                    for q in range(Q):
                        ins = pe.transpose(ps[:, 5 + c, P * q:P * (q + 1)], yn[t % 2][:, H * q + P * c:H * q + P * (c + 1)], ident[:, :])
                ins.then_inc(c_ps, 1)

            transpose_x(0)
            pe.wait_ge(prow_in, 48)
            pe.wait_ge(hot_ok, 1)
            for n in range(NPC):
                ins = pe.matmul(ps[:, 7, T * n:T * (n + 1)], prows[:, P * n:P * (n + 1)], hot[:, :], start=True, stop=True)
            ins.then_inc(pcol_ps, 1)
            for t in range(T):
                if t + 1 < T:
                    transpose_x(t + 1)
                project_down(t)
                project_up(t)
                if t >= 2:
                    transpose_y(t - 2)
            for t in range(T - 2, T):
                transpose_y(t)

            def turn_weight(m, lo, hi, bank):
                pe.wait_ge(wdeq_ok, m + 1)
                for n in range(lo, hi):
                    if m < 2:
                        c, j = n // IC, n % IC
                        src = wdeq[m][:, H * j + P * c:H * j + P * (c + 1)]
                    else:
                        j, c = n // HC, n % HC
                        src = wdeq[m][:, I * c + P * j:I * c + P * (j + 1)]
                    ins = pe.transpose(ps[:, bank + (n - lo) // 4, P * ((n - lo) % 4):P * ((n - lo) % 4 + 1)], src, ident[:, :])
                return ins

            turn_weight(0, 0, IC * HC, 0).then_inc(wT_ps, 1)

            rounds = [0]

            def spread_max(n):
                rounds[0] += 1
                pe.wait_ge(max_ok, rounds[0])
                for k in range(n):
                    ins = pe.transpose(ps[0:1, 7, P * k:P * (k + 1)], pm[:, k:k + 1], ident[:, :])
                ins.then_inc(maxT_ps, 1)
                pe.wait_ge(max_row, rounds[0])
                pe.matmul(ps[:, 7, 256:256 + n], ones[:, :], row[:, 0:n], start=True, stop=True).then_inc(max_bc, 1)

            spread_max(1)
            pe.wait_ge(pair_sb, 3)

            def project(wT, position, counted, pairs=range(NPAIR)):
                for q in pairs:
                    pe.wait_ge(pair_sb, NPAIR * counted + q + 1)
                    for j in (2 * q, 2 * q + 1):
                        for c in range(HC):
                            ins = pe.matmul(ps[:, j, :], wT[:, I * c + P * j:I * c + P * (j + 1)],
                                            ubuf[:, bass.ds(TE * position + S * c, S)], start=c == 0, stop=c == HC - 1)
                    ins.then_inc(pair_ps, 1)

            with pe.Fori(0, T - NTURN) as t:
                pe.wait_ge(cq_ok, t + 1)
                project(wgT, t, t)
            copied = 0
            for r in range(NTURN):
                if r:
                    pe.wait_ge(wT_sb, copied)
                for m, _, lo, hi, bank in turns[r]:
                    ins = turn_weight(m, lo, hi, bank)
                    copied += 1
                ins.then_inc(wT_ps, 1)
                pe.wait_ge(cq_ok, T - NTURN + r + 1)
                project(wgT, T - NTURN + r, T - NTURN + r)
            pe.wait_ge(wT_sb, copied)
            project(wuT, KEEP, T, range(1))
            spread_max(1)
            project(wuT, KEEP, T, range(1, NPAIR))
            with pe.Fori(1, KEEP) as n:
                project(wuT, KEEP + n, T + n)
            with pe.Fori(0, KEEP) as n:
                project(wuT, n, T + KEEP + n)
            spread_max(2)
            spread_max(1)

            def project_out(k, s):
                pe.wait_ge(oq32_ok, 4 * k + 2 * s + 2)
                for q in range(Q):
                    for j in range(IC):
                        ins = pe.matmul(ps[:, 2 * s + q // 2, H * (q % 2):H * (q % 2 + 1)],
                                        oq32[s][:, S * j + P * q:S * j + P * (q + 1)],
                                        wdT[:, H * j:H * (j + 1)], start=j == 0, stop=j == IC - 1)
                ins.then_inc(o_ps, 1)

            pe.wait_ge(pair_sb, 3 + 2 * T * NPAIR)
            for s in range(2):
                project_out(0, s)
            with pe.Fori(1, T // 2) as k:
                for s in range(2):
                    pe.wait_ge(o_sb, 2 * k + s - 1)
                    project_out(k, s)


_INS = ["x", "itok_B_0_6", "L0_cond_down_w", "L0_cond_down_b", "L0_cond_up_w", "L0_cond_up_b", "L0_cond_ln_g",
        "L0_cond_ln_b", "L0_ffn_w_gate", "L0_ffn_w_up", "L0_ffn_w_down"]


def kernel(**inputs):
    import numpy as np
    import concourse.bacc as bacc
    from concourse import mybir as mb
    from concourse.bass_utils import run_bass_kernel_spmd

    nc = bacc.Bacc("TRN2", target_bir_lowering=False, num_devices=1)
    arrays, args = {}, []
    for name in _INS:
        a = np.ascontiguousarray(inputs[name])
        arrays[f"in_{name}"] = a
        args.append(nc.dram_tensor(f"in_{name}", a.shape, mb.dt.from_np(a.dtype), kind="ExternalInput").ap())
    shape = inputs["x"].shape
    args.append(nc.dram_tensor("out_0", shape, mb.dt.float32, kind="ExternalOutput").ap())
    adaln_ffn_kernel(nc, *args)
    r = run_bass_kernel_spmd(nc, [arrays], core_ids=[0])
    return r.results[0]["out_0"]
```

```python
from contextlib import ExitStack

import concourse.bass as bass
from concourse import mybir

P = 128
F32 = mybir.dt.float32
I16 = mybir.dt.int16
I32 = mybir.dt.int32
ALU = mybir.AluOpType
ACT = mybir.ActivationFunctionType
AX = mybir.AxisListType

BLOCK = 32
W_QMAX = 7.0
A_QMAX = 32767.0
TINY = 1e-12
LN_EPS = 1e-5
SIG_STEPS = 65536.0
INT_ROUND = 1.5 * 2.0 ** 23


def adaln_ffn_kernel(nc, x, profile, down_w, down_b, up_w, up_b, ln_g, ln_b, w_gate, w_up, w_down, out):
    T, S, H = x.shape
    NPROF, _, K = down_w.shape
    I = w_gate.shape[0]
    Q = S // P
    HC, IC = H // P, I // P
    NPAIR = IC // 2
    TE = HC * S
    TI = IC * S
    HALF = TI // 2
    WN = HC * I
    KEEP = T // 2
    UPS_BESIDE_GATE, UMAX_BESIDE_GATE, SPREAD_H_AT, HABS_BESIDE_UP = 16, 11, 6, 6
    WARM = (7, 7, 4, 7, 5)
    assert S == 512 and K == P and IC % 2 == 0 and T % 4 == 0 and Q % 2 == 0

    x_t = x.rearrange("t (p q) h -> t p (q h)", q=Q)
    out_t = out.rearrange("t (p q) h -> t p (q h)", q=Q)
    spill = nc.dram_tensor("up_spill", [KEEP, P, TI], F32, kind="Internal").ap()

    with ExitStack() as ctx:
        def sb(name, shape, dt=F32):
            return ctx.enter_context(nc.sbuf_tensor(name, shape, dt))

        def sem(name):
            return ctx.enter_context(nc.semaphore(name))

        gbuf = sb("gbuf", [P, (T + 1) * TI])
        wgT = gbuf[:, 0:WN]
        CQ = T * TE
        UQ0 = CQ - HALF
        ubuf = sb("ubuf", [P, CQ + KEEP * TI])
        wuT = sb("wuT", [P, WN])
        wdT = sb("wdT", [P, WN])
        gint = sb("gint", [P, 2, HALF], I16)
        NPC = 1 + 2 * HC
        ids = sb("ids", [NPROF, T], I32)
        hot = sb("hot", [NPROF, T])
        prof_i = sb("prof_i", [NPROF, 1], I32)
        prof = sb("prof", [NPROF, 1])
        sc = sb("sc", [P, 32])
        mx = sb("mx", [P, 3 * T])
        mx2 = sb("mx2", [P, 2 * T + 1])
        top = sb("top", [P, T + 1])
        topi = sb("topi", [P, 1], I16)
        pm = sb("pm", [P, 2])
        row = sb("row", [1, 2])
        ones = sb("ones", [1, P])
        ident = sb("ident", [P, P])
        ps = ctx.enter_context(nc.psum_tensor("ps", [P, 8, 512], F32))

        h16 = gbuf[:, 0:T * TI].bitcast(I16)
        uq16 = ubuf[:, UQ0:UQ0 + T * HALF].bitcast(I16)

        def hq(t, half):
            return h16[:, bass.ds(2 * TI * t + HALF * half, HALF)]

        def habs(t):
            return h16[:, 2 * TI * t + TI:2 * TI * (t + 1)]

        def freed(t):
            return gbuf[:, TI * t + HALF:TI * (t + 1)]

        def gtile(t, half=None):
            o = TI * t + TI
            return gbuf[:, bass.ds(o, TI)] if half is None else gbuf[:, bass.ds(o + HALF * half, HALF)]

        def uslot(s):
            return ubuf[:, bass.ds(CQ + TI * s, TI)]

        at = [WN]

        def cut(buf, n):
            at[0] += n
            return buf[:, at[0] - n:at[0]]

        xs = [cut(gbuf, TE) for _ in range(T)]
        wd = [cut(gbuf, HC * K) for _ in range(T)]
        wu = [cut(gbuf, H) for _ in range(T)]
        bu = [cut(gbuf, H) for _ in range(T)]
        xT = [cut(gbuf, TE) for _ in range(2)]
        xb = [cut(gbuf, TE) for _ in range(2)]
        ys = [cut(gbuf, TE) for _ in range(2)]
        yn = [cut(gbuf, TE) for _ in range(2)]
        zT = [cut(gbuf, S) for _ in range(2)]
        prows = cut(gbuf, K + 2 * H)[0:NPROF, :]
        NB = WN // BLOCK
        wscale = cut(gbuf, 3 * 2 * NB).rearrange("p (m k n) -> p m k n", m=3, k=2)
        stats = cut(gbuf, 2 * Q * 6).rearrange("p (s q n) -> p s q n", s=2, q=Q)
        assert at[0] <= (T + 1) * TI
        at[0] = CQ
        wnat = [cut(ubuf, WN) for _ in range(3)]
        wdeq = [cut(ubuf, WN) for _ in range(3)]
        pcols = cut(ubuf, NPC * T).rearrange("p (n t) -> p n t", t=T)
        mv = cut(ubuf, 2 * Q * 2).rearrange("p (s q n) -> p s q n", s=2, q=Q)
        rstd, nmean, nmr = (cut(ubuf, 2 * Q).rearrange("p (s q) -> p s q", s=2) for _ in range(3))
        half_neg = cut(ubuf, Q)
        assert at[0] <= CQ + KEEP * TI

        assert HALF == WN
        turn16 = [wuT[:, :].bitcast(I16), gint[:, :, :].rearrange("p a n -> p (a n)")]
        oq32 = [ubuf[:, TI * s:TI * (s + 1)] for s in range(2)]
        xr = [freed(T - 4 + s)[:, 0:TE] for s in range(2)]
        ot = [freed(T - 2 + s)[:, 0:TE] for s in range(2)]
        assert 2 * TI <= UQ0 and TE <= HALF
        back = [[ubuf[:, 0:TI]], [ubuf[:, TI:2 * TI]], [freed(0), freed(1)], [freed(2), freed(3)]]
        assert T - KEEP == len(back)

        ids_in, prow_in = sem("ids_in"), sem("prow_in")
        x_in = [sem(f"x_in{t}") for t in range(T)]
        w_in = [sem(f"w_in{t}") for t in range(T)]
        wnat_in = [sem(f"wnat_in{m}") for m in range(3)]
        const_ok, hot_ok = sem("const_ok"), sem("hot_ok")
        pcol_ps, pcol_sb = sem("pcol_ps"), sem("pcol_sb")
        pow_ok, yn_half = sem("pow_ok"), sem("yn_half")
        xT_ps, xT_sb, z_ps, z_sb, y_ps, y_sb = (sem(n) for n in ("xT_ps", "xT_sb", "z_ps", "z_sb", "y_ps", "y_sb"))
        xb_ok, stat_ok, mv_ok, var_ok, rstd_ok, yn_ok = (sem(n) for n in ("xb_ok", "stat_ok", "mv_ok", "var_ok", "rstd_ok", "yn_ok"))
        c_ps, c_sb, cmax_ok = sem("c_ps"), sem("c_sb"), sem("cmax_ok")
        wamax_ok, wscale_ok, wwhole_ok, wint_ok, wdeq_ok, wT_ps, wT_sb = (
            sem(n) for n in ("wamax_ok", "wscale_ok", "wwhole_ok", "wint_ok", "wdeq_ok", "wT_ps", "wT_sb"))
        max_ok, maxT_ps, max_row, max_bc = (sem(n) for n in ("max_ok", "maxT_ps", "max_row", "max_bc"))
        calc = sem("calc")
        cround, cq_ok = sem("cround"), sem("cq_ok")
        pair_ps = sem("pair_ps")
        pair_sb = sem("pair_sb")
        gmax_ok, umax_ok = sem("gmax_ok"), sem("umax_ok")
        gtop_ok, top_ok, neg_ok = sem("gtop_ok"), sem("top_ok"), sem("neg_ok")
        kg_ok, kh_ok, ku_ok = sem("kg_ok"), sem("kh_ok"), sem("ku_ok")
        gint_ok, sig_ok, sigq_ok, h_ok = (sem(n) for n in ("gint_ok", "sig_ok", "sigq_ok", "h_ok"))
        spilled = sem("spilled")
        reload = [sem(f"reload{i}") for i in range(T - KEEP)]
        hq_ok, habs_ok, uq_ok, uabs_ok, omax_ok = (sem(n) for n in ("hq_ok", "habs_ok", "uq_ok", "uabs_ok", "omax_ok"))
        oq16_ok, oq32_ok, o_ps, o_sb = (sem(n) for n in ("oq16_ok", "oq32_ok", "o_ps", "o_sb"))
        xr_in = [sem(f"xr_in{s}") for s in range(2)]
        stored = [sem(f"stored{s}") for s in range(2)]

        turns = [[(1, wuT, 0, 8, 6)], [(1, wuT, 8, 12, 6), (2, wdT, 0, 4, 7)], [(2, wdT, 4, 12, 6)]]
        NTURN = len(turns)
        assert IC * HC == 12
        S_C, INV_C, S_G, K_G, S_U, K_U, S_H, K_H, S_HU, S_O, K_O, S_GS, NS_G, TMP = range(14)

        def col(k):
            return sc[:, k:k + 1]

        ctx.enter_context(nc.allow_non_contiguous_dma(reason="rows of biases"))
        block = ctx.enter_context(nc.Block())

        @block.sync
        def _(sp):
            sp.dma_start(ids[:, :], profile.rearrange("(a t) -> a t", a=1).to_broadcast([NPROF, T])).then_inc(ids_in, 16)
            sp.dma_start(xs[0], x_t[0]).then_inc(x_in[0], 16)
            sp.dma_start(prows[:, 0:K], down_b).then_inc(prow_in, 16)
            sp.dma_start(prows[:, K:K + H], ln_g).then_inc(prow_in, 16)
            sp.dma_start(prows[:, K + H:K + 2 * H], ln_b).then_inc(prow_in, 16)
            sp.wait_ge(ids_in, 16)
            for t in range(T):
                r = sp.value_load(ids[0:1, t:t + 1], min_val=0, max_val=NPROF - 1)
                sp.dma_start(wd[t].rearrange("p (c k) -> p c k", c=HC),
                             down_w[bass.ds(r, 1), :, :].rearrange("a (c p) k -> p (a c) k", p=P)).then_inc(w_in[t], 16)
                sp.dma_start(wu[t], up_w[bass.ds(r, 1), :, :].rearrange("a k h -> k (a h)")).then_inc(w_in[t], 16)
                sp.dma_start(bu[t], up_b[bass.ds(r, 1), :].to_broadcast([P, H])).then_inc(w_in[t], 16)
                if t + 1 < T:
                    sp.dma_start(xs[t + 1], x_t[t + 1]).then_inc(x_in[t + 1], 16)
                for m, (after, w) in enumerate(((0, w_gate), (T - 2, w_up), (T - 1, w_down))):
                    if t == after:
                        sp.dma_start(wnat[m].rearrange("p (c k) -> p c k", k=w.shape[1]),
                                     w.rearrange("(c p) k -> p c k", p=P)).then_inc(wnat_in[m], 16)
            for n in range(KEEP):
                sp.wait_ge(pair_sb, 3 + NPAIR * (T + 1 + n))
                sp.dma_start(spill[n], uslot(n)).then_inc(spilled, 16)
                sp.wait_ge(spilled, 16 * n + 16)
            sp.wait_ge(pair_ps, 2 * T * NPAIR)
            for i, places in enumerate(back):
                if len(places) > 1:
                    sp.wait_ge(omax_ok, 2 * (i - 1))
                for k, place in enumerate(places):
                    n = TI // len(places)
                    sp.dma_start(place, spill[i][:, n * k:n * (k + 1)]).then_inc(reload[i], 16)
            sp.wait_ge(omax_ok, T - 2)
            for s in range(2):
                sp.dma_start(xr[s], x_t[s]).then_inc(xr_in[s], 16)
            with sp.Fori(0, T // 2 - 1) as k:
                for s in range(2):
                    sp.wait_ge(o_sb, 2 * k + s + 1)
                    sp.wait_ge(omax_ok, T)
                    sp.dma_start(out_t[bass.ds(2 * k + s, 1)].rearrange("a p n -> p (a n)"), ot[s]).then_inc(stored[s], 16)
                    sp.dma_start(xr[s], x_t[bass.ds(2 * k + 2 + s, 1)].rearrange("a p n -> p (a n)")).then_inc(xr_in[s], 16)
            sp.wait_ge(o_sb, T - 1)
            sp.dma_start(out_t[T - 2], ot[0]).then_inc(stored[0], 16)
            for h in range(2):
                sp.wait_ge(o_sb, T + h)
                sp.dma_start(out_t[T - 1][:, S * h:S * (h + 1)], ot[1][:, S * h:S * (h + 1)]).then_inc(stored[1], 16)
            sp.wait_ge(stored[0], 16 * (T // 2))
            sp.wait_ge(stored[1], 16 * (T // 2 + 1))

        @block.gpsimd
        def _(pool):
            pool.memset(ones[:, :], 1.0).then_inc(const_ok, 1)
            pool.memset(ident[:, :], 0.0).then_inc(const_ok, 1)
            pool.wait_ge(const_ok, 2)
            pool.affine_select(out=ident[:, :], in_=ident[:, :], compare_op=ALU.not_equal, fill=1.0, base=0,
                               pattern=[[-1, P]], channel_multiplier=1).then_inc(const_ok, 1)
            pool.memset(half_neg[:, :], -0.5).then_inc(const_ok, 1)
            pool.iota(prof_i[:, :], pattern=[[0, 1]], base=0, channel_multiplier=1).then_inc(const_ok, 1)

            def add_bias(t):
                pool.wait_ge(x_in[t], 16)
                pool.wait_ge(w_in[t], 48)
                if t >= 2:
                    pool.wait_ge(y_sb, t - 1)
                pool.tensor_tensor(xb[t % 2].rearrange("p (q h) -> p q h", q=Q),
                                   xs[t].rearrange("p (q h) -> p q h", q=Q),
                                   bu[t].rearrange("p (a h) -> p a h", a=1).to_broadcast([P, Q, H]),
                                   ALU.add).then_inc(xb_ok, 1)

            def quantise_weight(m):
                pool.wait_ge(wscale_ok, m + 1)
                wide, fine = (v.rearrange("p (n b) -> p n b", b=BLOCK) for v in (wnat[m], wdeq[m]))
                s, inv = (wscale[:, m, k, :].rearrange("p (n a) -> p n a", a=1).to_broadcast([P, NB, BLOCK]) for k in (0, 1))
                pool.tensor_tensor(fine, wide, inv, ALU.mult).then_inc(wint_ok, 1)
                pool.wait_ge(wint_ok, 3 * m - 2)
                pool.tensor_scalar(wdeq[m], wdeq[m], 1.0, INT_ROUND, ALU.mult, ALU.add).then_inc(wint_ok, 1)
                pool.wait_ge(wint_ok, 3 * m - 1)
                pool.tensor_scalar(wdeq[m], wdeq[m], -INT_ROUND, 1.0, ALU.add, ALU.mult).then_inc(wint_ok, 1)
                pool.wait_ge(wint_ok, 3 * m)
                pool.tensor_tensor(fine, fine, s, ALU.mult).then_inc(wdeq_ok, 1)

            add_bias(0)
            add_bias(1)
            for t in range(T):
                pool.wait_ge(var_ok, t + 1)
                pool.tensor_tensor(rstd[:, t % 2, :], rstd[:, t % 2, :], half_neg[:, :], ALU.pow).then_inc(pow_ok, 1)
                pool.wait_ge(pow_ok, t + 1)
                pool.tensor_tensor(nmr[:, t % 2, :], nmean[:, t % 2, :], rstd[:, t % 2, :], ALU.mult).then_inc(rstd_ok, 1)
                if t + 2 < T:
                    add_bias(t + 2)
            quantise_weight(1)
            quantise_weight(2)

            pool.wait_ge(kg_ok, 1)
            for g in range(2 * T):
                if g >= 2:
                    pool.wait_ge(h_ok, g - 1)
                pool.tensor_scalar(gint[:, g % 2, :], gtile(g // 2, g % 2), col(K_G), -1.0, ALU.mult, ALU.mult)\
                    .then_inc(gint_ok, 1)
            pool.wait_ge(top_ok, 1)
            pool.tensor_scalar(topi[:, :], top[:, T:T + 1], col(K_G), -1.0, ALU.mult, ALU.mult).then_inc(gint_ok, 1)

            pool.wait_ge(kh_ok, 1)
            for t in range(T):
                if t:
                    pool.wait_ge(hq_ok, t)
                    pool.wait_ge(habs_ok, t)
                pool.tensor_scalar(h16[:, 2 * TI * t:2 * TI * t + TI], gtile(t), col(K_H), -1.0, ALU.mult, ALU.mult)\
                    .then_inc(hq_ok, 1)

            pool.wait_ge(ku_ok, 1)
            done = 0
            for t in range(T):
                if t >= KEEP:
                    pool.wait_ge(reload[t - KEEP], 16 * len(back[t - KEEP]))
                if t:
                    pool.wait_ge(uq_ok, done)
                    pool.wait_ge(uabs_ok, done)
                at_ = 0
                for src in ([uslot(t)] if t < KEEP else back[t - KEEP]):
                    n = src.shape[1]
                    pool.tensor_scalar(uq16[:, TI * t + at_:TI * t + at_ + n], src, col(K_U), 1.0, ALU.mult, ALU.mult)\
                        .then_inc(uq_ok, 1)
                    at_ += n
                    done += 1

        @block.scalar
        def _(act):
            def copy_xT(t):
                act.wait_ge(xT_ps, t + 1)
                if t >= 2:
                    act.wait_ge(z_ps, t - 1)
                act.activation(xT[t % 2], ps[:, 0:HC, :], ACT.Copy).then_inc(xT_sb, 1)

            def relu_z(t):
                act.wait_ge(z_ps, t + 1)
                if t >= 2:
                    act.wait_ge(y_ps, t - 1)
                act.activation(zT[t % 2], ps[:, 2, :], ACT.Relu, bias=pcols[:, 0, t:t + 1]).then_inc(z_sb, 1)

            def scale_c(t):
                act.wait_ge(c_ps, t + 1)
                for c in range(HC):
                    act.activation(ubuf[:, TE * t + S * c:TE * t + S * (c + 1)], ps[:, 5 + c, :], ACT.Identity,
                                   scale=pcols[:, 1 + c, t:t + 1], bias=pcols[:, 1 + HC + c, t:t + 1]).then_inc(c_sb, 1)

            copy_xT(0)
            act.wait_ge(pcol_ps, 1)
            act.activation(pcols[:, :, :], ps[:, 7, 0:NPC * T].rearrange("p (n t) -> p n t", t=T), ACT.Copy).then_inc(pcol_sb, 1)
            act.wait_ge(pcol_sb, 1)

            def normalise(t, blocks):
                act.wait_ge(rstd_ok, t + 1)
                if t >= 2:
                    act.wait_ge(c_ps, t - 1)
                for q in blocks:
                    ins = act.activation(yn[t % 2][:, H * q:H * (q + 1)], ys[t % 2][:, H * q:H * (q + 1)], ACT.Identity,
                                         scale=rstd[:, t % 2, q:q + 1], bias=nmr[:, t % 2, q:q + 1])
                ins.then_inc(yn_ok, 1)

            for t in range(T):
                relu_z(t)
                if t >= 2:
                    scale_c(t - 2)
                if t + 1 < T:
                    copy_xT(t + 1)
                if t >= 1:
                    normalise(t - 1, range(Q))
            scale_c(T - 2)
            normalise(T - 1, range(Q // 2))
            scale_c(T - 1)

            def copy_weights(r):
                act.wait_ge(wT_ps, r + 2)
                for _, wT, lo, hi, bank in turns[r]:
                    banks = (hi - lo) // 4
                    act.activation(wT[:, P * lo:P * hi], ps[:, bank:bank + banks, :].rearrange("p b n -> p (b n)"),
                                   ACT.Copy).then_inc(wT_sb, 1)

            def copy_gate(t):
                for q in range(NPAIR):
                    act.wait_ge(pair_ps, NPAIR * t + q + 1)
                    act.wait_ge(max_bc, 1)
                    act.activation(gbuf[:, bass.ds(TI + TI * t + 2 * S * q, 2 * S)], ps[:, 2 * q:2 * q + 2, :],
                                   ACT.Copy).then_inc(pair_sb, 1)

            act.wait_ge(wT_ps, 1)
            for b in range(NPAIR):
                act.activation(wgT[:, 4 * P * b:4 * P * (b + 1)], ps[:, b, :], ACT.Copy).then_inc(pair_sb, 1)
            with act.Fori(0, T - NTURN) as t:
                copy_gate(t)
            for r in range(NTURN):
                copy_weights(r)
                copy_gate(T - NTURN + r)

            def copy_up(n):
                k, q = n // NPAIR, n % NPAIR
                act.wait_ge(pair_ps, NPAIR * T + n + 1)
                if k >= KEEP and q == 0:
                    act.wait_ge(spilled, 16 * (k - KEEP + 1))
                    act.wait_ge(umax_ok, NPAIR * (k - KEEP + 1))
                o = CQ + TI * (k % KEEP) + 2 * S * q
                act.activation(ubuf[:, o:o + 2 * S], ps[:, 2 * q:2 * q + 2, :], ACT.Copy).then_inc(pair_sb, 1)

            def gate_sigmoid(g):
                act.wait_ge(gint_ok, g + 1)
                if g == 0:
                    act.wait_ge(neg_ok, 1)
                if g == 2 * T - 2:
                    act.wait_ge(gtop_ok, T)
                act.activation(gtile(g // 2, g % 2), gint[:, g % 2, :], ACT.Sigmoid, scale=col(NS_G)).then_inc(sig_ok, 1)

            def abs_h(t):
                if t == 0:
                    act.wait_ge(kh_ok, 1)
                else:
                    act.wait_ge(hq_ok, t)
                    act.wait_ge(habs_ok, t)
                act.activation(habs(t), gtile(t), ACT.Abs, scale=col(K_H)).then_inc(habs_ok, 1)

            ups = 0
            for g in range(2 * T):
                while ups < (g + 1) * UPS_BESIDE_GATE // (2 * T):
                    copy_up(ups)
                    ups += 1
                gate_sigmoid(g)
            act.wait_ge(gint_ok, 2 * T + 1)
            act.activation(top[:, T:T + 1], topi[:, :], ACT.Sigmoid, scale=col(NS_G)).then_inc(sig_ok, 1)
            heads = 0
            while ups < T * NPAIR:
                copy_up(ups)
                ups += 1
                if ups >= T * NPAIR - HABS_BESIDE_UP + 1:
                    abs_h(heads)
                    heads += 1

            done = 0
            for t in range(T):
                if t == 0:
                    act.wait_ge(ku_ok, 1)
                if t >= KEEP:
                    act.wait_ge(reload[t - KEEP], 16 * len(back[t - KEEP]))
                if t >= 2:
                    act.wait_ge(omax_ok, t - 1)
                at_ = 0
                for src in ([uslot(t)] if t < KEEP else back[t - KEEP]):
                    n = src.shape[1]
                    act.activation(turn16[t % 2][:, at_:at_ + n], src, ACT.Abs, scale=col(K_U)).then_inc(uabs_ok, 1)
                    at_ += n
                if heads < T:
                    abs_h(heads)
                    heads += 1

            def widen(k, s):
                o, i = (v.rearrange("p (j n) -> p j n", j=IC) for v in (oq32[s], turn16[s]))
                for q in range(Q):
                    act.wait_ge(oq16_ok, 2 * Q * k + Q * s + q + 1)
                    act.activation(o[:, :, P * q:P * (q + 1)], i[:, :, P * q:P * (q + 1)], ACT.Copy).then_inc(oq32_ok, 1)

            for s in range(2):
                widen(0, s)
            with act.Fori(1, T // 2) as k:
                for s in range(2):
                    act.wait_ge(o_ps, 4 * k + 2 * s - 2)
                    widen(k, s)

        @block.vector
        def _(dve):
            count = [0]

            def small(ins):
                count[0] += 1
                ins.then_inc(calc, 1)
                dve.wait_ge(calc, count[0])

            def reduce_abs(o, i):
                return dve.tensor_reduce(o, i, AX.X, ALU.max, apply_absolute_value=True)

            rounds = [0]

            def global_max(sources):
                rounds[0] += 1
                for k, s in enumerate(sources):
                    small(dve.reduce_max(pm[:, k:k + 1], s, AX.X))
                dve.sem_inc(max_ok, 1)
                dve.wait_ge(maxT_ps, rounds[0])
                n = len(sources)
                dve.tensor_reduce(row[:, 0:n], ps[0:1, 7, 0:n * P].rearrange("a (n p) -> a n p", p=P), AX.X,
                                  ALU.max).then_inc(max_row, 1)
                dve.wait_ge(max_bc, rounds[0])
                return [ps[:, 7, 256 + k:257 + k] for k in range(n)]

            def scale_factor(maximum, unit, s_, k_, last=None):
                small(dve.tensor_scalar(col(TMP), maximum, col(unit), 1.0 / A_QMAX, ALU.mult, ALU.mult))
                small(dve.tensor_scalar(col(s_), col(TMP), TINY, None, ALU.max))
                small(dve.reciprocal(col(TMP), col(s_)))
                ins = dve.tensor_scalar(col(k_), col(TMP), col(unit), None, ALU.mult)
                if last is None:
                    small(ins)
                else:
                    ins.then_inc(last, 1)

            dve.wait_ge(const_ok, 5)
            dve.wait_ge(ids_in, 16)
            small(dve.tensor_copy(prof[:, :], prof_i[:, :]))
            dve.tensor_scalar(hot[:, :], ids[:, :], prof[:, 0:1], None, ALU.is_equal).then_inc(hot_ok, 1)

            def weight_scales(m):
                dve.wait_ge(wnat_in[m], 16)
                reduce_abs(wscale[:, m, 1, :], wnat[m].rearrange("p (n b) -> p n b", b=BLOCK)).then_inc(wamax_ok, 1)
                dve.wait_ge(wamax_ok, m + 1)
                small(dve.tensor_scalar(wscale[:, m, 0, :], wscale[:, m, 1, :], 1.0 / W_QMAX, TINY, ALU.mult, ALU.max))
                dve.reciprocal(wscale[:, m, 1, :], wscale[:, m, 0, :]).then_inc(wscale_ok, 1)

            def gate_weights(step):
                wide, whole, fine = (v.rearrange("p (n b) -> p n b", b=BLOCK) for v in (wnat[0], gint[:, 0, :], wdeq[0]))
                ws, winv = (wscale[:, 0, k, :].rearrange("p (n a) -> p n a", a=1).to_broadcast([P, NB, BLOCK]) for k in (0, 1))
                if step == 0:
                    weight_scales(0)
                if step == 1:
                    dve.wait_ge(wscale_ok, 1)
                    dve.tensor_tensor(whole, wide, winv, ALU.mult).then_inc(wwhole_ok, 1)
                if step == 2:
                    dve.wait_ge(wwhole_ok, 1)
                    dve.tensor_tensor(fine, whole, ws, ALU.mult).then_inc(wdeq_ok, 1)

            def take_cmax(t):
                dve.wait_ge(c_sb, HC * (t + 1))
                reduce_abs(mx[:, t:t + 1], ubuf[:, TE * t:TE * (t + 1)]).then_inc(cmax_ok, 1)

            for t in range(T):
                s = t % 2
                dve.wait_ge(y_ps, t + 1)
                dve.wait_ge(xb_ok, t + 1)
                if t >= 2:
                    dve.wait_ge(yn_ok, t - 1)
                dve.tensor_tensor(ys[s], ps[:, 3:5, :].rearrange("p a n -> p (a n)"), xb[s], ALU.add).then_inc(y_sb, 1)
                dve.wait_ge(y_sb, t + 1)
                for q in range(Q):
                    dve.bn_stats(stats[:, s, q, :], ys[s][:, H * q:H * (q + 1)]).then_inc(stat_ok, 1)
                for q in range(Q):
                    dve.wait_ge(stat_ok, Q * t + q + 1)
                    ins = dve.bn_aggr(mv[:, s, q, :], stats[:, s, q, :])
                ins.then_inc(mv_ok, 1)
                dve.wait_ge(mv_ok, t + 1)
                dve.tensor_scalar(nmean[:, s, :], mv[:, s, :, 0], -1.0, None, ALU.mult)
                dve.tensor_scalar(rstd[:, s, :], mv[:, s, :, 1], LN_EPS, None, ALU.add).then_inc(var_ok, 1)
                gate_weights(t)
                if t >= 3:
                    take_cmax(t - 3)
            dve.wait_ge(rstd_ok, T)
            for q in range(Q // 2, Q):
                ins = dve.tensor_scalar(yn[s][:, H * q:H * (q + 1)], ys[s][:, H * q:H * (q + 1)],
                                        mv[:, s, q, 0:1], rstd[:, s, q:q + 1], ALU.subtract, ALU.mult)
            ins.then_inc(yn_half, 1)
            for t in range(T - 3, T - 1):
                take_cmax(t)
            for c in range(HC):
                dve.wait_ge(c_sb, HC * (T - 1) + c + 1)
                reduce_abs(mx[:, T - 1 + c:T + c], ubuf[:, TE * (T - 1) + S * c:TE * (T - 1) + S * (c + 1)])\
                    .then_inc(cmax_ok, 1)

            dve.wait_ge(cmax_ok, T - 1 + HC)
            cmax, = global_max([mx[:, 0:T - 1 + HC]])
            small(dve.tensor_scalar(col(S_C), cmax, 1.0 / A_QMAX, TINY, ALU.mult, ALU.max))
            small(dve.reciprocal(col(INV_C), col(S_C)))
            with dve.Fori(0, T) as t:
                ct = ubuf[:, bass.ds(TE * t, TE)]
                dve.tensor_scalar(ct, ct, col(INV_C), INT_ROUND, ALU.mult, ALU.add).then_inc(cround, 1)
                dve.wait_ge(cround, t + 1)
                dve.tensor_scalar(ct, ct, INT_ROUND, None, ALU.subtract).then_inc(cq_ok, 1)
            for m in (1, 2):
                weight_scales(m)
            def take_gmax(t):
                for q in range(NPAIR):
                    dve.wait_ge(pair_sb, 3 + NPAIR * t + q + 1)
                    reduce_abs(mx[:, bass.ds(NPAIR * t + q, 1)],
                               gbuf[:, bass.ds(TI + TI * t + 2 * S * q, 2 * S)]).then_inc(gmax_ok, 1)

            def take_top(t):
                dve.reduce_max(top[:, bass.ds(t, 1)], gtile(t), AX.X).then_inc(gtop_ok, 1)

            with dve.Fori(0, T - 1) as t:
                take_gmax(t)
                take_top(t)
            take_gmax(T - 1)
            dve.wait_ge(gmax_ok, NPAIR * T)
            gmax, = global_max([mx[:, 0:NPAIR * T]])
            scale_factor(gmax, S_C, S_G, K_G, kg_ok)
            dve.tensor_scalar(col(NS_G), col(S_G), -1.0, None, ALU.mult).then_inc(neg_ok, 1)
            take_top(T - 1)
            dve.wait_ge(gtop_ok, T)
            dve.reduce_max(top[:, T:T + 1], top[:, 0:T], AX.X).then_inc(top_ok, 1)

            def take_umax(n):
                k, q = n // NPAIR, n % NPAIR
                dve.wait_ge(pair_sb, 3 + NPAIR * T + n + 1)
                o = CQ + TI * (k % KEEP) + 2 * S * q
                reduce_abs(mx[:, n:n + 1], ubuf[:, o:o + 2 * S]).then_inc(umax_ok, 1)

            taken = 0
            for g in range(2 * T):
                gt = gtile(g // 2, g % 2)
                dve.wait_ge(sig_ok, g + 1)
                dve.tensor_scalar(gt.bitcast(I32), gt, SIG_STEPS, SIG_STEPS - 1.0, ALU.mult, ALU.min).then_inc(sigq_ok, 1)
                dve.wait_ge(sigq_ok, g + 1)
                dve.tensor_tensor_reduce(out=gt, in0=gt.bitcast(I32), in1=gint[:, g % 2, :], scale=1.0, scalar=0.0,
                                         op0=ALU.mult, op1=ALU.max, accum_out=mx2[:, g:g + 1]).then_inc(h_ok, 1)
                while taken < (g + 1) * UMAX_BESIDE_GATE // (2 * T):
                    take_umax(taken)
                    taken += 1
            dve.wait_ge(sig_ok, 2 * T + 1)
            small(dve.tensor_scalar(top[:, 0:1].bitcast(I32), top[:, T:T + 1], SIG_STEPS, SIG_STEPS - 1.0, ALU.mult, ALU.min))
            small(dve.scalar_tensor_tensor(mx2[:, 2 * T:2 * T + 1], top[:, 0:1].bitcast(I32), -1.0, topi[:, :],
                                           ALU.mult, ALU.mult))
            small(dve.tensor_scalar(col(S_GS), col(S_G), 1.0 / SIG_STEPS, None, ALU.mult))
            dve.wait_ge(h_ok, 2 * T)
            hmax, = global_max([mx2[:, 0:2 * T + 1]])
            scale_factor(hmax, S_GS, S_H, K_H, kh_ok)
            for n in range(taken, NPAIR * T):
                take_umax(n)
            dve.wait_ge(umax_ok, NPAIR * T)
            umax, = global_max([mx[:, 0:NPAIR * T]])
            scale_factor(umax, S_C, S_U, K_U, ku_ok)

            pieces = 0
            for t in range(T):
                pieces += 1 if t < KEEP else len(back[t - KEEP])
                dve.wait_ge(habs_ok, t + 1)
                dve.wait_ge(uabs_ok, pieces)
                if t >= 1:
                    dve.wait_ge(omax_ok, t)
                dve.tensor_tensor_reduce(out=ps[:, 0:IC, :].rearrange("p b n -> p (b n)"), in0=habs(t), in1=turn16[t % 2],
                                         scale=1.0, scalar=0.0, op0=ALU.mult, op1=ALU.max,
                                         accum_out=mx2[:, t:t + 1]).then_inc(omax_ok, 1)
            dve.wait_ge(omax_ok, T)
            small(dve.tensor_scalar(col(S_HU), col(S_H), col(S_U), None, ALU.mult))
            omax, = global_max([mx2[:, 0:T]])
            scale_factor(omax, S_HU, S_O, K_O)

            def round_product(t, s):
                a, b = h16[:, bass.ds(2 * TI * t, TI)], uq16[:, bass.ds(TI * t, TI)]
                for q in range(Q):
                    o, i, j = (v.rearrange("p (j n) -> p j n", j=IC)[:, :, P * q:P * (q + 1)] for v in (turn16[s], a, b))
                    dve.scalar_tensor_tensor(o, i, col(K_O), j, ALU.mult, ALU.mult).then_inc(oq16_ok, 1)

            def add_residual(k, s, wait_stored=True):
                t = 2 * k + s
                dve.wait_ge(o_ps, 2 * t + 2)
                dve.wait_ge(xr_in[s], 16 * k + 16)
                if wait_stored:
                    dve.wait_ge(stored[s], 16 * k)
                dve.scalar_tensor_tensor(ot[s], ps[:, 2 * s:2 * s + 2, :].rearrange("p a n -> p (a n)"), col(S_O),
                                         xr[s], ALU.mult, ALU.add).then_inc(o_sb, 1)

            dve.wait_ge(hq_ok, T)
            dve.wait_ge(uq_ok, pieces)
            for s in range(2):
                round_product(s, s)
            for s in range(2):
                dve.wait_ge(oq32_ok, Q * (s + 1))
                round_product(2 + s, s)
                add_residual(0, s, wait_stored=False)
            with dve.Fori(1, T // 2 - 1) as k:
                for s in range(2):
                    dve.wait_ge(oq32_ok, 2 * Q * k + Q * (s + 1))
                    round_product(2 * k + 2 + s, s)
                    add_residual(k, s)
            add_residual(T // 2 - 1, 0)
            for h in range(2):
                dve.wait_ge(o_ps, 2 * T - 1 + h)
                dve.wait_ge(xr_in[1], 16 * (T // 2))
                dve.wait_ge(stored[1], 16 * (T // 2 - 1))
                dve.scalar_tensor_tensor(ot[1][:, S * h:S * (h + 1)], ps[:, 2 + h, :], col(S_O), xr[1][:, S * h:S * (h + 1)],
                                         ALU.mult, ALU.add).then_inc(o_sb, 1)

        @block.tensor
        def _(pe):
            def keep_clock(n, bank=6):
                for k in range(n):
                    pe.matmul(ps[:, bank, 0:P], ident[:, :], ident[:, :], start=k == 0, stop=k == n - 1)

            pe.wait_ge(const_ok, 5)
            keep_clock(WARM[0])

            def transpose_x(t):
                pe.wait_ge(x_in[t], 16)
                if t >= 1:
                    pe.wait_ge(xT_sb, t)
                for c in range(HC):
                    for q in range(Q):
                        ins = pe.transpose(ps[:, c, P * q:P * (q + 1)], xs[t][:, H * q + P * c:H * q + P * (c + 1)], ident[:, :])
                ins.then_inc(xT_ps, 1)

            def project_down(t):
                pe.wait_ge(w_in[t], 48)
                pe.wait_ge(xT_sb, t + 1)
                if t >= 1:
                    pe.wait_ge(z_sb, t)
                for c in range(HC):
                    ins = pe.matmul(ps[:, 2, :], wd[t][:, K * c:K * (c + 1)], xT[t % 2][:, S * c:S * (c + 1)],
                                    start=c == 0, stop=c == HC - 1)
                ins.then_inc(z_ps, 1)

            def project_up(t):
                pe.wait_ge(z_sb, t + 1)
                if t >= 1:
                    pe.wait_ge(y_sb, t)
                for q in range(Q):
                    ins = pe.matmul(ps[:, 3 + q // 2, H * (q % 2):H * (q % 2 + 1)], zT[t % 2][:, P * q:P * (q + 1)],
                                    wu[t], start=True, stop=True)
                ins.then_inc(y_ps, 1)

            def transpose_y(t):
                pe.wait_ge(yn_ok, t + 1)
                if t == T - 1:
                    pe.wait_ge(yn_half, 1)
                if t >= 1:
                    pe.wait_ge(c_sb, HC * t)
                for c in range(HC):
                    for q in range(Q):
                        ins = pe.transpose(ps[:, 5 + c, P * q:P * (q + 1)], yn[t % 2][:, H * q + P * c:H * q + P * (c + 1)], ident[:, :])
                ins.then_inc(c_ps, 1)

            transpose_x(0)
            pe.wait_ge(prow_in, 48)
            pe.wait_ge(hot_ok, 1)
            for n in range(NPC):
                ins = pe.matmul(ps[:, 7, T * n:T * (n + 1)], prows[:, P * n:P * (n + 1)], hot[:, :], start=True, stop=True)
            ins.then_inc(pcol_ps, 1)
            for t in range(T):
                project_down(t)
                if t >= 2:
                    transpose_y(t - 2)
                if t + 1 < T:
                    transpose_x(t + 1)
                project_up(t)
            transpose_y(T - 2)

            def turn_weight(m, lo, hi, bank):
                pe.wait_ge(wdeq_ok, m + 1)
                for n in range(lo, hi):
                    if m < 2:
                        c, j = n // IC, n % IC
                        src = wdeq[m][:, H * j + P * c:H * j + P * (c + 1)]
                    else:
                        j, c = n // HC, n % HC
                        src = wdeq[m][:, I * c + P * j:I * c + P * (j + 1)]
                    ins = pe.transpose(ps[:, bank + (n - lo) // 4, P * ((n - lo) % 4):P * ((n - lo) % 4 + 1)], src, ident[:, :])
                return ins

            turn_weight(0, 0, IC * HC, 0).then_inc(wT_ps, 1)
            keep_clock(WARM[1], bank=7)
            transpose_y(T - 1)

            rounds = [0]

            def spread_max(n):
                rounds[0] += 1
                pe.wait_ge(max_ok, rounds[0])
                for k in range(n):
                    ins = pe.transpose(ps[0:1, 7, P * k:P * (k + 1)], pm[:, k:k + 1], ident[:, :])
                ins.then_inc(maxT_ps, 1)
                pe.wait_ge(max_row, rounds[0])
                pe.matmul(ps[:, 7, 256:256 + n], ones[:, :], row[:, 0:n], start=True, stop=True).then_inc(max_bc, 1)

            spread_max(1)
            keep_clock(WARM[2])
            pe.wait_ge(pair_sb, 3)

            def project(wT, position, counted, pairs=range(NPAIR)):
                for q in pairs:
                    pe.wait_ge(pair_sb, NPAIR * counted + q + 1)
                    for j in (2 * q, 2 * q + 1):
                        for c in range(HC):
                            ins = pe.matmul(ps[:, j, :], wT[:, I * c + P * j:I * c + P * (j + 1)],
                                            ubuf[:, bass.ds(TE * position + S * c, S)], start=c == 0, stop=c == HC - 1)
                    ins.then_inc(pair_ps, 1)

            with pe.Fori(0, T - NTURN) as t:
                pe.wait_ge(cq_ok, t + 1)
                project(wgT, t, t)
            copied = 0
            for r in range(NTURN):
                if r:
                    pe.wait_ge(wT_sb, copied)
                for m, _, lo, hi, bank in turns[r]:
                    ins = turn_weight(m, lo, hi, bank)
                    copied += 1
                ins.then_inc(wT_ps, 1)
                pe.wait_ge(cq_ok, T - NTURN + r + 1)
                project(wgT, T - NTURN + r, T - NTURN + r)
            pe.wait_ge(wT_sb, copied)
            project(wuT, KEEP, T, range(1))
            spread_max(1)
            project(wuT, KEEP, T, range(1, NPAIR))
            with pe.Fori(1, KEEP) as n:
                project(wuT, KEEP + n, T + n)
            at_h = SPREAD_H_AT - KEEP
            with pe.Fori(0, at_h) as n:
                project(wuT, n, T + KEEP + n)
            project(wuT, at_h, T + KEEP + at_h, range(1))
            spread_max(1)
            project(wuT, at_h, T + KEEP + at_h, range(1, NPAIR))
            for n in range(at_h + 1, KEEP):
                project(wuT, n, T + KEEP + n)
            spread_max(1)
            pe.wait_ge(omax_ok, T - 1)
            keep_clock(WARM[3])
            spread_max(1)
            keep_clock(WARM[4])

            def project_out(k, s):
                for q in range(Q):
                    pe.wait_ge(oq32_ok, 2 * Q * k + Q * s + q + 1)
                    for j in range(IC):
                        ins = pe.matmul(ps[:, 2 * s + q // 2, H * (q % 2):H * (q % 2 + 1)],
                                        oq32[s][:, S * j + P * q:S * j + P * (q + 1)],
                                        wdT[:, H * j:H * (j + 1)], start=j == 0, stop=j == IC - 1)
                    if q % 2:
                        ins.then_inc(o_ps, 1)

            pe.wait_ge(pair_sb, 3 + 2 * T * NPAIR)
            for s in range(2):
                project_out(0, s)
            with pe.Fori(1, T // 2) as k:
                for s in range(2):
                    pe.wait_ge(o_sb, 2 * k + s - 1)
                    project_out(k, s)


_INS = ["x", "itok_B_0_6", "L0_cond_down_w", "L0_cond_down_b", "L0_cond_up_w", "L0_cond_up_b", "L0_cond_ln_g",
        "L0_cond_ln_b", "L0_ffn_w_gate", "L0_ffn_w_up", "L0_ffn_w_down"]


def kernel(**inputs):
    import numpy as np
    import concourse.bacc as bacc
    from concourse import mybir as mb
    from concourse.bass_utils import run_bass_kernel_spmd

    nc = bacc.Bacc("TRN2", target_bir_lowering=False, num_devices=1)
    arrays, args = {}, []
    for name in _INS:
        a = np.ascontiguousarray(inputs[name])
        arrays[f"in_{name}"] = a
        args.append(nc.dram_tensor(f"in_{name}", a.shape, mb.dt.from_np(a.dtype), kind="ExternalInput").ap())
    shape = inputs["x"].shape
    args.append(nc.dram_tensor("out_0", shape, mb.dt.float32, kind="ExternalOutput").ap())
    adaln_ffn_kernel(nc, *args)
    r = run_bass_kernel_spmd(nc, [arrays], core_ids=[0])
    return r.results[0]["out_0"]
```

```python
from contextlib import ExitStack

import concourse.bass as bass
from concourse import mybir

P = 128
F32 = mybir.dt.float32
I16 = mybir.dt.int16
I32 = mybir.dt.int32
ALU = mybir.AluOpType
ACT = mybir.ActivationFunctionType
AX = mybir.AxisListType

BLOCK = 32
W_QMAX = 7.0
A_QMAX = 32767.0
TINY = 1e-12
LN_EPS = 1e-5
SIG_STEPS = 65536.0
INT_ROUND = 1.5 * 2.0 ** 23


def adaln_ffn_kernel(nc, x, profile, down_w, down_b, up_w, up_b, ln_g, ln_b, w_gate, w_up, w_down, out):
    T, S, H = x.shape
    NPROF, _, K = down_w.shape
    I = w_gate.shape[0]
    Q = S // P
    HC, IC = H // P, I // P
    NPAIR = IC // 2
    TE = HC * S
    TI = IC * S
    HALF = TI // 2
    WN = HC * I
    KEEP = T // 2
    UPS_BESIDE_GATE, UMAX_BESIDE_GATE, SPREAD_H_AT = 15, 7, 17
    HABS_AFTER_COPY = {0: 17, 1: 17, 3: 19, 4: 20, 5: 21, 6: 21, 7: 24}
    HABS_AFTER_UMAX = {2: 14, 5: 19}
    TOP_AT = 4
    ACT_BLOCKS = 3
    WARM = (7, 10, 10, 5, 8, 6)
    LAST_PIECES, LAST_BANKS = ((0, 2), (2, 3), (3, 4)), (2, 2, 3, 4)
    assert S == 512 and Q == 4 and K == P and IC % 2 == 0 and T % 4 == 0

    x_t = x.rearrange("t (p q) h -> t p (q h)", q=Q)
    out_t = out.rearrange("t (p q) h -> t p (q h)", q=Q)
    spill = nc.dram_tensor("up_spill", [KEEP, P, TI], F32, kind="Internal").ap()

    with ExitStack() as ctx:
        def sb(name, shape, dt=F32):
            return ctx.enter_context(nc.sbuf_tensor(name, shape, dt))

        def sem(name):
            return ctx.enter_context(nc.semaphore(name))

        gbuf = sb("gbuf", [P, (T + 1) * TI])
        wgT = gbuf[:, 0:WN]
        CQ = T * TE
        UQ0 = CQ - HALF
        ubuf = sb("ubuf", [P, CQ + KEEP * TI])
        wuT = sb("wuT", [P, WN])
        wdT = sb("wdT", [P, WN])
        gint = sb("gint", [P, 2, HALF], I16)
        NPC = 1 + 2 * HC
        ids = sb("ids", [NPROF, T], I32)
        hot = sb("hot", [NPROF, T])
        prof_i = sb("prof_i", [NPROF, 1], I32)
        prof = sb("prof", [NPROF, 1])
        sc = sb("sc", [P, 32])
        mx = sb("mx", [P, NPAIR * T])
        mx2 = sb("mx2", [P, 2 * T + 1])
        top = sb("top", [P, T + 1])
        topi = sb("topi", [P, 1], I16)
        pm = sb("pm", [P, 2])
        row = sb("row", [1, 2])
        ones = sb("ones", [1, P])
        ident = sb("ident", [P, P])
        ps = ctx.enter_context(nc.psum_tensor("ps", [P, 8, 512], F32))

        h16 = gbuf[:, 0:T * TI].bitcast(I16)
        uq16 = ubuf[:, UQ0:UQ0 + T * HALF].bitcast(I16)

        def habs(t):
            return h16[:, 2 * TI * t + TI:2 * TI * (t + 1)]

        def freed(t):
            return gbuf[:, TI * t + HALF:TI * (t + 1)]

        def gtile(t, half=None):
            o = TI * t + TI
            return gbuf[:, bass.ds(o, TI)] if half is None else gbuf[:, bass.ds(o + HALF * half, HALF)]

        def uslot(s):
            return ubuf[:, bass.ds(CQ + TI * s, TI)]

        at = [WN]

        def cut(buf, n):
            at[0] += n
            return buf[:, at[0] - n:at[0]]

        xs = [cut(gbuf, TE) for _ in range(T)]
        wd = [cut(gbuf, HC * K) for _ in range(T)]
        wu = [cut(gbuf, H) for _ in range(T)]
        bu = [cut(gbuf, H) for _ in range(T)]
        xT = [cut(gbuf, TE) for _ in range(2)]
        xb = [cut(gbuf, TE) for _ in range(2)]
        ys = [cut(gbuf, TE) for _ in range(2)]
        yn = [cut(gbuf, TE) for _ in range(2)]
        zT = [cut(gbuf, S) for _ in range(2)]
        prows = cut(gbuf, K + 2 * H)[0:NPROF, :]
        NB = WN // BLOCK
        wscale = cut(gbuf, 3 * 2 * NB).rearrange("p (m k n) -> p m k n", m=3, k=2)
        stats = cut(gbuf, 2 * Q * 6).rearrange("p (s q n) -> p s q n", s=2, q=Q)
        assert at[0] <= (T + 1) * TI
        at[0] = CQ
        wnat = [cut(ubuf, WN) for _ in range(3)]
        wdeq = [cut(ubuf, WN) for _ in range(3)]
        pcols = cut(ubuf, NPC * T).rearrange("p (n t) -> p n t", t=T)
        mv = cut(ubuf, 2 * Q * 2).rearrange("p (s q n) -> p s q n", s=2, q=Q)
        rstd, nmean, nmr = (cut(ubuf, 2 * Q).rearrange("p (s q) -> p s q", s=2) for _ in range(3))
        half_neg = cut(ubuf, Q)
        assert at[0] <= CQ + KEEP * TI

        gap = gbuf[:, WN:TI].bitcast(I16)
        gring = [gint[:, 0, :], gint[:, 1, :], gap[:, 0:HALF], gap[:, HALF:2 * HALF]]
        RING = len(gring)
        assert HALF == WN
        turn16 = [wuT[:, :].bitcast(I16), gint[:, :, :].rearrange("p a n -> p (a n)")]
        oq32 = [ubuf[:, TI * s:TI * (s + 1)] for s in range(2)]
        xr = [freed(T - 4 + s)[:, 0:TE] for s in range(2)]
        ot = [freed(T - 2 + s)[:, 0:TE] for s in range(2)]
        assert 2 * TI <= UQ0 and TE <= HALF
        back = [[ubuf[:, 0:TI]], [ubuf[:, TI:2 * TI]], [freed(0), freed(1)], [freed(2), freed(3)]]
        assert T - KEEP == len(back)

        def pieces_of(t):
            if t >= KEEP:
                return back[t - KEEP]
            return [uslot(0)[:, HALF * h:HALF * (h + 1)] for h in range(2)] if t == 0 else [uslot(t)]

        ends = [sum(len(pieces_of(i)) for i in range(t + 1)) for t in range(T)]

        ids_in, prow_in = sem("ids_in"), sem("prow_in")
        x_in = [sem(f"x_in{t}") for t in range(T)]
        w_in = [sem(f"w_in{t}") for t in range(T)]
        wnat_in = [sem(f"wnat_in{m}") for m in range(3)]
        const_ok, hot_ok = sem("const_ok"), sem("hot_ok")
        pcol_ps, pcol_sb = sem("pcol_ps"), sem("pcol_sb")
        pow_ok, yn2_ok = sem("pow_ok"), sem("yn2_ok")
        xT_ps, xT_sb, z_ps, z_sb, y_ps, y_sb = (sem(n) for n in ("xT_ps", "xT_sb", "z_ps", "z_sb", "y_ps", "y_sb"))
        xb_ok, stat_ok, mv_ok, var_ok, rstd_ok, yn_ok = (sem(n) for n in ("xb_ok", "stat_ok", "mv_ok", "var_ok", "rstd_ok", "yn_ok"))
        c_ps, c_sb, cmax_ok = sem("c_ps"), sem("c_sb"), sem("cmax_ok")
        wamax_ok, wscale_ok, wwhole_ok, wint_ok, wdeq_ok, wT_ps, wT_sb = (
            sem(n) for n in ("wamax_ok", "wscale_ok", "wwhole_ok", "wint_ok", "wdeq_ok", "wT_ps", "wT_sb"))
        max_ok, maxT_ps, max_row, max_bc = (sem(n) for n in ("max_ok", "maxT_ps", "max_row", "max_bc"))
        calc = sem("calc")
        cround, cq_ok = sem("cround"), sem("cq_ok")
        pair_ps = sem("pair_ps")
        pair_sb = sem("pair_sb")
        gmax_ok, umax_ok = sem("gmax_ok"), sem("umax_ok")
        gtop_ok, top_ok, topi_ok, topsig_ok, neg_ok = (sem(n) for n in ("gtop_ok", "top_ok", "topi_ok", "topsig_ok", "neg_ok"))
        kg_ok, kh_ok, ku_ok = sem("kg_ok"), sem("kh_ok"), sem("ku_ok")
        gint_ok, sig_ok, sigq_ok, h_ok = (sem(n) for n in ("gint_ok", "sig_ok", "sigq_ok", "h_ok"))
        spilled = sem("spilled")
        reload = [sem(f"reload{i}") for i in range(T - KEEP)]
        hq_ok, habs_ok, habs2_ok, uq_ok, uabs_ok, omax_ok = (
            sem(n) for n in ("hq_ok", "habs_ok", "habs2_ok", "uq_ok", "uabs_ok", "omax_ok"))
        oq16_ok, oq32_ok, o_ps, o_sb = (sem(n) for n in ("oq16_ok", "oq32_ok", "o_ps", "o_sb"))
        xr_in = [sem(f"xr_in{s}") for s in range(2)]
        stored = [sem(f"stored{s}") for s in range(2)]

        turns = [[(1, wuT, 0, 8, 6)], [(1, wuT, 8, 12, 6), (2, wdT, 0, 4, 7)], [(2, wdT, 4, 12, 6)]]
        NTURN = len(turns)
        assert IC * HC == 12
        S_C, INV_C, S_G, K_G, S_U, K_U, S_H, K_H, S_HU, S_O, K_O, S_GS, NS_G, TMP = range(14)

        def col(k):
            return sc[:, k:k + 1]

        ctx.enter_context(nc.allow_non_contiguous_dma(reason="rows of biases"))
        block = ctx.enter_context(nc.Block())

        @block.sync
        def _(sp):
            sp.dma_start(ids[:, :], profile.rearrange("(a t) -> a t", a=1).to_broadcast([NPROF, T])).then_inc(ids_in, 16)
            sp.dma_start(xs[0], x_t[0]).then_inc(x_in[0], 16)
            sp.dma_start(prows[:, 0:K], down_b).then_inc(prow_in, 16)
            sp.dma_start(prows[:, K:K + H], ln_g).then_inc(prow_in, 16)
            sp.dma_start(prows[:, K + H:K + 2 * H], ln_b).then_inc(prow_in, 16)
            sp.wait_ge(ids_in, 16)
            for t in range(T):
                r = sp.value_load(ids[0:1, t:t + 1], min_val=0, max_val=NPROF - 1)
                sp.dma_start(wd[t].rearrange("p (c k) -> p c k", c=HC),
                             down_w[bass.ds(r, 1), :, :].rearrange("a (c p) k -> p (a c) k", p=P)).then_inc(w_in[t], 16)
                sp.dma_start(wu[t], up_w[bass.ds(r, 1), :, :].rearrange("a k h -> k (a h)")).then_inc(w_in[t], 16)
                sp.dma_start(bu[t], up_b[bass.ds(r, 1), :].to_broadcast([P, H])).then_inc(w_in[t], 16)
                if t + 1 < T:
                    sp.dma_start(xs[t + 1], x_t[t + 1]).then_inc(x_in[t + 1], 16)
                for m, (after, w) in enumerate(((0, w_gate), (T - 2, w_up), (T - 1, w_down))):
                    if t == after:
                        sp.dma_start(wnat[m].rearrange("p (c k) -> p c k", k=w.shape[1]),
                                     w.rearrange("(c p) k -> p c k", p=P)).then_inc(wnat_in[m], 16)
            for n in range(KEEP):
                sp.wait_ge(pair_sb, 3 + NPAIR * (T + 1 + n))
                sp.dma_start(spill[n], uslot(n)).then_inc(spilled, 16)
                sp.wait_ge(spilled, 16 * n + 16)
            sp.wait_ge(pair_ps, 2 * T * NPAIR)
            for i, places in enumerate(back):
                if len(places) > 1:
                    sp.wait_ge(omax_ok, 2 * (i - 1) + 1)
                for k, place in enumerate(places):
                    n = TI // len(places)
                    sp.dma_start(place, spill[i][:, n * k:n * (k + 1)]).then_inc(reload[i], 16)
            sp.wait_ge(omax_ok, T - 1)
            for s in range(2):
                sp.dma_start(xr[s], x_t[s]).then_inc(xr_in[s], 16)
            with sp.Fori(0, T // 2 - 1) as k:
                for s in range(2):
                    sp.wait_ge(o_sb, 2 * k + s + 1)
                    sp.wait_ge(omax_ok, T + 1)
                    sp.dma_start(out_t[bass.ds(2 * k + s, 1)].rearrange("a p n -> p (a n)"), ot[s]).then_inc(stored[s], 16)
                    sp.dma_start(xr[s], x_t[bass.ds(2 * k + 2 + s, 1)].rearrange("a p n -> p (a n)")).then_inc(xr_in[s], 16)
            sp.wait_ge(o_sb, T - 1)
            sp.dma_start(out_t[T - 2], ot[0]).then_inc(stored[0], 16)
            for n, (lo, hi) in enumerate(LAST_PIECES):
                sp.wait_ge(o_sb, T + n)
                sp.dma_start(out_t[T - 1][:, H * lo:H * hi], ot[1][:, H * lo:H * hi]).then_inc(stored[1], 16)
            sp.wait_ge(stored[0], 16 * (T // 2))
            sp.wait_ge(stored[1], 16 * (T // 2 - 1 + len(LAST_PIECES)))

        @block.gpsimd
        def _(pool):
            pool.memset(ones[:, :], 1.0).then_inc(const_ok, 1)
            pool.memset(ident[:, :], 0.0).then_inc(const_ok, 1)
            pool.wait_ge(const_ok, 2)
            pool.affine_select(out=ident[:, :], in_=ident[:, :], compare_op=ALU.not_equal, fill=1.0, base=0,
                               pattern=[[-1, P]], channel_multiplier=1).then_inc(const_ok, 1)
            pool.memset(half_neg[:, :], -0.5).then_inc(const_ok, 1)
            pool.iota(prof_i[:, :], pattern=[[0, 1]], base=0, channel_multiplier=1).then_inc(const_ok, 1)

            def add_bias(t):
                pool.wait_ge(x_in[t], 16)
                pool.wait_ge(w_in[t], 48)
                if t >= 2:
                    pool.wait_ge(y_sb, t - 1)
                pool.tensor_tensor(xb[t % 2].rearrange("p (q h) -> p q h", q=Q),
                                   xs[t].rearrange("p (q h) -> p q h", q=Q),
                                   bu[t].rearrange("p (a h) -> p a h", a=1).to_broadcast([P, Q, H]),
                                   ALU.add).then_inc(xb_ok, 1)

            def quantise_weight(m):
                pool.wait_ge(wscale_ok, m + 1)
                wide, fine = (v.rearrange("p (n b) -> p n b", b=BLOCK) for v in (wnat[m], wdeq[m]))
                s, inv = (wscale[:, m, k, :].rearrange("p (n a) -> p n a", a=1).to_broadcast([P, NB, BLOCK]) for k in (0, 1))
                pool.tensor_tensor(fine, wide, inv, ALU.mult).then_inc(wint_ok, 1)
                pool.wait_ge(wint_ok, 3 * m - 2)
                pool.tensor_scalar(wdeq[m], wdeq[m], 1.0, INT_ROUND, ALU.mult, ALU.add).then_inc(wint_ok, 1)
                pool.wait_ge(wint_ok, 3 * m - 1)
                pool.tensor_scalar(wdeq[m], wdeq[m], -INT_ROUND, 1.0, ALU.add, ALU.mult).then_inc(wint_ok, 1)
                pool.wait_ge(wint_ok, 3 * m)
                pool.tensor_tensor(fine, fine, s, ALU.mult).then_inc(wdeq_ok, 1)

            add_bias(0)
            add_bias(1)
            for t in range(T):
                pool.wait_ge(var_ok, t + 1)
                pool.tensor_tensor(rstd[:, t % 2, :], rstd[:, t % 2, :], half_neg[:, :], ALU.pow).then_inc(pow_ok, 1)
                pool.wait_ge(pow_ok, t + 1)
                pool.tensor_tensor(nmr[:, t % 2, :], nmean[:, t % 2, :], rstd[:, t % 2, :], ALU.mult).then_inc(rstd_ok, 1)
                if t + 2 < T:
                    add_bias(t + 2)
            quantise_weight(1)
            quantise_weight(2)

            pool.wait_ge(kg_ok, 1)
            for g in range(2 * T):
                if g >= RING:
                    pool.wait_ge(h_ok, g - RING + 1)
                pool.tensor_scalar(gring[g % RING], gtile(g // 2, g % 2), col(K_G), -1.0, ALU.mult, ALU.mult)\
                    .then_inc(gint_ok, 1)
                if g == TOP_AT:
                    pool.wait_ge(top_ok, 1)
                    pool.tensor_scalar(topi[:, :], top[:, T:T + 1], col(K_G), -1.0, ALU.mult, ALU.mult).then_inc(topi_ok, 1)

            pool.wait_ge(kh_ok, 1)
            for t in range(T):
                if t:
                    pool.wait_ge(hq_ok, t)
                    pool.wait_ge(habs_ok, sum(i < t for i in HABS_AFTER_COPY))
                pool.tensor_scalar(h16[:, 2 * TI * t:2 * TI * t + TI], gtile(t), col(K_H), -1.0, ALU.mult, ALU.mult)\
                    .then_inc(hq_ok, 1)

            pool.wait_ge(ku_ok, 1)
            done = 0
            for t in range(T):
                if t >= KEEP:
                    pool.wait_ge(reload[t - KEEP], 16 * len(back[t - KEEP]))
                if t:
                    pool.wait_ge(uq_ok, done)
                    pool.wait_ge(uabs_ok, done)
                at_ = 0
                for src in pieces_of(t):
                    n = src.shape[1]
                    pool.tensor_scalar(uq16[:, TI * t + at_:TI * t + at_ + n], src, col(K_U), 1.0, ALU.mult, ALU.mult)\
                        .then_inc(uq_ok, 1)
                    at_ += n
                    done += 1

        @block.scalar
        def _(act):
            def copy_xT(t):
                act.wait_ge(xT_ps, t + 1)
                if t >= 2:
                    act.wait_ge(z_ps, t - 1)
                act.activation(xT[t % 2], ps[:, 0:HC, :], ACT.Copy).then_inc(xT_sb, 1)

            def relu_z(t):
                act.wait_ge(z_ps, t + 1)
                if t >= 2:
                    act.wait_ge(y_ps, t - 1)
                act.activation(zT[t % 2], ps[:, 2, :], ACT.Relu, bias=pcols[:, 0, t:t + 1]).then_inc(z_sb, 1)

            def scale_c(t):
                act.wait_ge(c_ps, t + 1)
                for c in range(HC):
                    act.activation(ubuf[:, TE * t + S * c:TE * t + S * (c + 1)], ps[:, 5 + c, :], ACT.Identity,
                                   scale=pcols[:, 1 + c, t:t + 1], bias=pcols[:, 1 + HC + c, t:t + 1]).then_inc(c_sb, 1)

            copy_xT(0)
            act.wait_ge(pcol_ps, 1)
            act.activation(pcols[:, :, :], ps[:, 7, 0:NPC * T].rearrange("p (n t) -> p n t", t=T), ACT.Copy).then_inc(pcol_sb, 1)
            act.wait_ge(pcol_sb, 1)

            def normalise(t, blocks):
                act.wait_ge(rstd_ok, t + 1)
                if t >= 2:
                    act.wait_ge(c_ps, t - 1)
                for q in blocks:
                    ins = act.activation(yn[t % 2][:, H * q:H * (q + 1)], ys[t % 2][:, H * q:H * (q + 1)], ACT.Identity,
                                         scale=rstd[:, t % 2, q:q + 1], bias=nmr[:, t % 2, q:q + 1])
                ins.then_inc(yn_ok, 1)

            for t in range(T):
                relu_z(t)
                if t >= 2:
                    scale_c(t - 2)
                if t + 1 < T:
                    copy_xT(t + 1)
                if t >= 1:
                    normalise(t - 1, range(ACT_BLOCKS))
            scale_c(T - 2)
            normalise(T - 1, range(Q // 2))
            scale_c(T - 1)

            def copy_weights(r):
                act.wait_ge(wT_ps, r + 2)
                for _, wT, lo, hi, bank in turns[r]:
                    banks = (hi - lo) // 4
                    act.activation(wT[:, P * lo:P * hi], ps[:, bank:bank + banks, :].rearrange("p b n -> p (b n)"),
                                   ACT.Copy).then_inc(wT_sb, 1)

            def copy_gate(t):
                for q in range(NPAIR):
                    act.wait_ge(pair_ps, NPAIR * t + q + 1)
                    act.wait_ge(max_bc, 1)
                    act.activation(gbuf[:, bass.ds(TI + TI * t + 2 * S * q, 2 * S)], ps[:, 2 * q:2 * q + 2, :],
                                   ACT.Copy).then_inc(pair_sb, 1)

            act.wait_ge(wT_ps, 1)
            for b in range(NPAIR):
                act.activation(wgT[:, 4 * P * b:4 * P * (b + 1)], ps[:, b, :], ACT.Copy).then_inc(pair_sb, 1)
            with act.Fori(0, T - NTURN) as t:
                copy_gate(t)
            for r in range(NTURN):
                copy_weights(r)
                copy_gate(T - NTURN + r)

            def copy_up(n):
                k, q = n // NPAIR, n % NPAIR
                act.wait_ge(pair_ps, NPAIR * T + n + 1)
                if k >= KEEP and q == 0:
                    act.wait_ge(spilled, 16 * (k - KEEP + 1))
                    act.wait_ge(umax_ok, NPAIR * (k - KEEP + 1))
                o = CQ + TI * (k % KEEP) + 2 * S * q
                act.activation(ubuf[:, o:o + 2 * S], ps[:, 2 * q:2 * q + 2, :], ACT.Copy).then_inc(pair_sb, 1)

            def gate_sigmoid(g):
                act.wait_ge(gint_ok, g + 1)
                if g == 0:
                    act.wait_ge(neg_ok, 1)
                if g == 2 * T - 2:
                    act.wait_ge(gtop_ok, T)
                act.activation(gtile(g // 2, g % 2), gring[g % RING], ACT.Sigmoid, scale=col(NS_G)).then_inc(sig_ok, 1)

            def abs_h(t):
                if t == 0:
                    act.wait_ge(kh_ok, 1)
                else:
                    act.wait_ge(hq_ok, t)
                    act.wait_ge(habs_ok, sum(i < t for i in HABS_AFTER_COPY))
                o = HALF if t in HABS_AFTER_UMAX else 0
                act.activation(habs(t)[:, o:TI], gtile(t)[:, o:TI], ACT.Abs, scale=col(K_H)).then_inc(habs_ok, 1)

            ups = 0
            for g in range(2 * T):
                while ups < (g + 1) * UPS_BESIDE_GATE // (2 * T):
                    copy_up(ups)
                    ups += 1
                gate_sigmoid(g)
                if g == TOP_AT:
                    act.wait_ge(topi_ok, 1)
                    act.activation(top[:, T:T + 1], topi[:, :], ACT.Sigmoid, scale=col(NS_G)).then_inc(topsig_ok, 1)
            while ups < T * NPAIR:
                copy_up(ups)
                ups += 1
                for t, after in HABS_AFTER_COPY.items():
                    if after == ups:
                        abs_h(t)

            act.wait_ge(ku_ok, 1)
            for t in range(T):
                if t >= KEEP:
                    act.wait_ge(reload[t - KEEP], 16 * len(back[t - KEEP]))
                if t >= 2:
                    act.wait_ge(omax_ok, t)
                at_ = 0
                for src in pieces_of(t):
                    n = src.shape[1]
                    act.activation(turn16[t % 2][:, at_:at_ + n], src, ACT.Abs, scale=col(K_U)).then_inc(uabs_ok, 1)
                    at_ += n

            def widen(k, s):
                o, i = (v.rearrange("p (j n) -> p j n", j=IC) for v in (oq32[s], turn16[s]))
                for q in range(Q):
                    act.wait_ge(oq16_ok, 2 * Q * k + Q * s + q + 1)
                    act.activation(o[:, :, P * q:P * (q + 1)], i[:, :, P * q:P * (q + 1)], ACT.Copy).then_inc(oq32_ok, 1)

            for s in range(2):
                widen(0, s)
            with act.Fori(1, T // 2) as k:
                for s in range(2):
                    act.wait_ge(o_ps, 8 * k + 4 * s - 4)
                    widen(k, s)

        @block.vector
        def _(dve):
            count = [0]

            def small(ins):
                count[0] += 1
                ins.then_inc(calc, 1)
                dve.wait_ge(calc, count[0])

            def reduce_abs(o, i):
                return dve.tensor_reduce(o, i, AX.X, ALU.max, apply_absolute_value=True)

            rounds = [0]

            def global_max(sources):
                rounds[0] += 1
                for k, s in enumerate(sources):
                    small(dve.reduce_max(pm[:, k:k + 1], s, AX.X))
                dve.sem_inc(max_ok, 1)
                dve.wait_ge(maxT_ps, rounds[0])
                n = len(sources)
                dve.tensor_reduce(row[:, 0:n], ps[0:1, 7, 0:n * P].rearrange("a (n p) -> a n p", p=P), AX.X,
                                  ALU.max).then_inc(max_row, 1)
                dve.wait_ge(max_bc, rounds[0])
                return [ps[:, 7, 256 + k:257 + k] for k in range(n)]

            def scale_factor(maximum, unit, s_, k_, last=None):
                small(dve.tensor_scalar(col(TMP), maximum, col(unit), 1.0 / A_QMAX, ALU.mult, ALU.mult))
                small(dve.tensor_scalar(col(s_), col(TMP), TINY, None, ALU.max))
                small(dve.reciprocal(col(TMP), col(s_)))
                ins = dve.tensor_scalar(col(k_), col(TMP), col(unit), None, ALU.mult)
                if last is None:
                    small(ins)
                else:
                    ins.then_inc(last, 1)

            dve.wait_ge(const_ok, 5)
            dve.wait_ge(ids_in, 16)
            small(dve.tensor_copy(prof[:, :], prof_i[:, :]))
            dve.tensor_scalar(hot[:, :], ids[:, :], prof[:, 0:1], None, ALU.is_equal).then_inc(hot_ok, 1)

            def weight_scales(m):
                dve.wait_ge(wnat_in[m], 16)
                reduce_abs(wscale[:, m, 1, :], wnat[m].rearrange("p (n b) -> p n b", b=BLOCK)).then_inc(wamax_ok, 1)
                dve.wait_ge(wamax_ok, m + 1)
                small(dve.tensor_scalar(wscale[:, m, 0, :], wscale[:, m, 1, :], 1.0 / W_QMAX, TINY, ALU.mult, ALU.max))
                dve.reciprocal(wscale[:, m, 1, :], wscale[:, m, 0, :]).then_inc(wscale_ok, 1)

            def gate_weights(step):
                wide, whole, fine = (v.rearrange("p (n b) -> p n b", b=BLOCK) for v in (wnat[0], gint[:, 0, :], wdeq[0]))
                ws, winv = (wscale[:, 0, k, :].rearrange("p (n a) -> p n a", a=1).to_broadcast([P, NB, BLOCK]) for k in (0, 1))
                if step == 0:
                    weight_scales(0)
                if step == 1:
                    dve.wait_ge(wscale_ok, 1)
                    dve.tensor_tensor(whole, wide, winv, ALU.mult).then_inc(wwhole_ok, 1)
                if step == 2:
                    dve.wait_ge(wwhole_ok, 1)
                    dve.tensor_tensor(fine, whole, ws, ALU.mult).then_inc(wdeq_ok, 1)

            def normalise(t, blocks):
                s = t % 2
                dve.wait_ge(rstd_ok, t + 1)
                if t >= 2:
                    dve.wait_ge(c_ps, t - 1)
                for q in blocks:
                    ins = dve.tensor_scalar(yn[s][:, H * q:H * (q + 1)], ys[s][:, H * q:H * (q + 1)],
                                            mv[:, s, q, 0:1], rstd[:, s, q:q + 1], ALU.subtract, ALU.mult)
                ins.then_inc(yn2_ok, 1)

            def take_cmax(t):
                dve.wait_ge(c_sb, HC * (t + 1))
                reduce_abs(mx[:, t:t + 1], ubuf[:, TE * t:TE * (t + 1)]).then_inc(cmax_ok, 1)

            for t in range(T):
                s = t % 2
                dve.wait_ge(y_ps, t + 1)
                dve.wait_ge(xb_ok, t + 1)
                if t >= 2:
                    dve.wait_ge(yn_ok, t - 1)
                    dve.wait_ge(yn2_ok, t - 1)
                if t < T - 1:
                    dve.tensor_tensor(ys[s], ps[:, 3:5, :].rearrange("p a n -> p (a n)"), xb[s], ALU.add).then_inc(y_sb, 1)
                    dve.wait_ge(y_sb, t + 1)
                for q in range(Q):
                    if t == T - 1 and q % 2 == 0:
                        dve.wait_ge(y_ps, T + q // 2)
                        dve.tensor_tensor(ys[s][:, H * q:H * (q + 2)], ps[:, 3 + q // 2, :], xb[s][:, H * q:H * (q + 2)],
                                          ALU.add).then_inc(y_sb, 1)
                        dve.wait_ge(y_sb, T + q // 2)
                    dve.bn_stats(stats[:, s, q, :], ys[s][:, H * q:H * (q + 1)]).then_inc(stat_ok, 1)
                for q in range(Q):
                    dve.wait_ge(stat_ok, Q * t + q + 1)
                    ins = dve.bn_aggr(mv[:, s, q, :], stats[:, s, q, :])
                ins.then_inc(mv_ok, 1)
                dve.wait_ge(mv_ok, t + 1)
                dve.tensor_scalar(nmean[:, s, :], mv[:, s, :, 0], -1.0, None, ALU.mult)
                dve.tensor_scalar(rstd[:, s, :], mv[:, s, :, 1], LN_EPS, None, ALU.add).then_inc(var_ok, 1)
                gate_weights(t)
                if t >= 3:
                    take_cmax(t - 3)
                if t < T - 1:
                    normalise(t, range(ACT_BLOCKS, Q))
            normalise(T - 1, range(Q // 2, Q))
            for t in range(T - 3, T - 1):
                take_cmax(t)
            for c in range(HC):
                dve.wait_ge(c_sb, HC * (T - 1) + c + 1)
                reduce_abs(mx[:, T - 1 + c:T + c], ubuf[:, TE * (T - 1) + S * c:TE * (T - 1) + S * (c + 1)])\
                    .then_inc(cmax_ok, 1)

            dve.wait_ge(cmax_ok, T - 1 + HC)
            cmax, = global_max([mx[:, 0:T - 1 + HC]])
            small(dve.tensor_scalar(col(S_C), cmax, 1.0 / A_QMAX, TINY, ALU.mult, ALU.max))
            small(dve.reciprocal(col(INV_C), col(S_C)))
            for c in range(HC):
                ct = ubuf[:, S * c:S * (c + 1)]
                small(dve.tensor_scalar(ct, ct, col(INV_C), INT_ROUND, ALU.mult, ALU.add))
                dve.tensor_scalar(ct, ct, INT_ROUND, None, ALU.subtract).then_inc(cq_ok, 1)
            with dve.Fori(1, T) as t:
                ct = ubuf[:, bass.ds(TE * t, TE)]
                dve.tensor_scalar(ct, ct, col(INV_C), INT_ROUND, ALU.mult, ALU.add).then_inc(cround, 1)
                dve.wait_ge(cround, t)
                dve.tensor_scalar(ct, ct, INT_ROUND, None, ALU.subtract).then_inc(cq_ok, 1)
            for m in (1, 2):
                weight_scales(m)

            def take_gmax(t):
                for q in range(NPAIR):
                    dve.wait_ge(pair_sb, 3 + NPAIR * t + q + 1)
                    reduce_abs(mx[:, bass.ds(NPAIR * t + q, 1)],
                               gbuf[:, bass.ds(TI + TI * t + 2 * S * q, 2 * S)]).then_inc(gmax_ok, 1)

            def take_top(t):
                dve.reduce_max(top[:, bass.ds(t, 1)], gtile(t), AX.X).then_inc(gtop_ok, 1)

            with dve.Fori(0, T - 1) as t:
                take_gmax(t)
                take_top(t)
            take_gmax(T - 1)
            dve.wait_ge(gmax_ok, NPAIR * T)
            gmax, = global_max([mx[:, 0:NPAIR * T]])
            scale_factor(gmax, S_C, S_G, K_G, kg_ok)
            dve.tensor_scalar(col(NS_G), col(S_G), -1.0, None, ALU.mult).then_inc(neg_ok, 1)
            take_top(T - 1)
            dve.wait_ge(gtop_ok, T)
            dve.reduce_max(top[:, T:T + 1], top[:, 0:T], AX.X).then_inc(top_ok, 1)

            def take_umax(n):
                k, q = n // NPAIR, n % NPAIR
                dve.wait_ge(pair_sb, 3 + NPAIR * T + n + 1)
                o = CQ + TI * (k % KEEP) + 2 * S * q
                reduce_abs(mx[:, n:n + 1], ubuf[:, o:o + 2 * S]).then_inc(umax_ok, 1)

            taken = 0
            for g in range(2 * T):
                gt = gtile(g // 2, g % 2)
                dve.wait_ge(sig_ok, g + 1)
                dve.tensor_scalar(gt.bitcast(I32), gt, SIG_STEPS, SIG_STEPS - 1.0, ALU.mult, ALU.min).then_inc(sigq_ok, 1)
                dve.wait_ge(sigq_ok, g + 1)
                dve.tensor_tensor_reduce(out=gt, in0=gt.bitcast(I32), in1=gring[g % RING], scale=1.0, scalar=0.0,
                                         op0=ALU.mult, op1=ALU.max, accum_out=mx2[:, g:g + 1]).then_inc(h_ok, 1)
                while taken < g * UMAX_BESIDE_GATE // (2 * T - 1):
                    take_umax(taken)
                    taken += 1
                if g == TOP_AT:
                    dve.wait_ge(topsig_ok, 1)
                    small(dve.tensor_scalar(top[:, 0:1].bitcast(I32), top[:, T:T + 1], SIG_STEPS, SIG_STEPS - 1.0, ALU.mult, ALU.min))
                    small(dve.scalar_tensor_tensor(mx2[:, 2 * T:2 * T + 1], top[:, 0:1].bitcast(I32), -1.0, topi[:, :],
                                                   ALU.mult, ALU.mult))
                    small(dve.tensor_scalar(col(S_GS), col(S_G), 1.0 / SIG_STEPS, None, ALU.mult))
            dve.wait_ge(h_ok, 2 * T)
            hmax, = global_max([mx2[:, 0:2 * T + 1]])
            scale_factor(hmax, S_GS, S_H, K_H, kh_ok)
            for pair in range(taken, NPAIR * T):
                take_umax(pair)
                for t, after in HABS_AFTER_UMAX.items():
                    if after == pair + 1:
                        dve.wait_ge(hq_ok, t + 1)
                        n = HALF if t in HABS_AFTER_COPY else TI
                        whole = h16[:, 2 * TI * t:2 * TI * t + n]
                        dve.scalar_tensor_tensor(habs(t)[:, 0:n], whole, -1.0, whole, ALU.mult, ALU.max).then_inc(habs2_ok, 1)
            dve.wait_ge(umax_ok, NPAIR * T)
            umax, = global_max([mx[:, 0:NPAIR * T]])
            scale_factor(umax, S_C, S_U, K_U, ku_ok)

            for n in range(T + 1):
                t, o, w = (0, HALF * n, HALF) if n < 2 else (n - 1, 0, TI)
                if t in HABS_AFTER_COPY:
                    dve.wait_ge(habs_ok, list(HABS_AFTER_COPY).index(t) + 1)
                if t in HABS_AFTER_UMAX:
                    dve.wait_ge(habs2_ok, list(HABS_AFTER_UMAX).index(t) + 1)
                dve.wait_ge(uabs_ok, 1 if n == 0 else ends[t])
                if n:
                    dve.wait_ge(omax_ok, n)
                dve.tensor_tensor_reduce(out=ps[:, 0:IC, :].rearrange("p b n -> p (b n)")[:, 0:w],
                                         in0=habs(t)[:, o:o + w], in1=turn16[t % 2][:, o:o + w],
                                         scale=1.0, scalar=0.0, op0=ALU.mult, op1=ALU.max,
                                         accum_out=mx2[:, n:n + 1]).then_inc(omax_ok, 1)
            dve.wait_ge(omax_ok, T + 1)
            small(dve.tensor_scalar(col(S_HU), col(S_H), col(S_U), None, ALU.mult))
            omax, = global_max([mx2[:, 0:T + 1]])
            scale_factor(omax, S_HU, S_O, K_O)

            def round_product(t, s):
                a, b = h16[:, bass.ds(2 * TI * t, TI)], uq16[:, bass.ds(TI * t, TI)]
                for q in range(Q):
                    o, i, j = (v.rearrange("p (j n) -> p j n", j=IC)[:, :, P * q:P * (q + 1)] for v in (turn16[s], a, b))
                    dve.scalar_tensor_tensor(o, i, col(K_O), j, ALU.mult, ALU.mult).then_inc(oq16_ok, 1)

            def add_residual(k, s, wait_stored=True):
                t = 2 * k + s
                dve.wait_ge(o_ps, 4 * t + 4)
                dve.wait_ge(xr_in[s], 16 * k + 16)
                if wait_stored:
                    dve.wait_ge(stored[s], 16 * k)
                dve.scalar_tensor_tensor(ot[s], ps[:, 2 * s:2 * s + 2, :].rearrange("p a n -> p (a n)"), col(S_O),
                                         xr[s], ALU.mult, ALU.add).then_inc(o_sb, 1)

            dve.wait_ge(hq_ok, T)
            dve.wait_ge(uq_ok, ends[T - 1])
            for s in range(2):
                round_product(s, s)
            for s in range(2):
                dve.wait_ge(oq32_ok, Q * (s + 1))
                round_product(2 + s, s)
                add_residual(0, s, wait_stored=False)
            with dve.Fori(1, T // 2 - 1) as k:
                for s in range(2):
                    dve.wait_ge(oq32_ok, 2 * Q * k + Q * (s + 1))
                    round_product(2 * k + 2 + s, s)
                    add_residual(k, s)
            add_residual(T // 2 - 1, 0)
            for lo, hi in LAST_PIECES:
                dve.wait_ge(o_ps, Q * (T - 1) + hi)
                dve.wait_ge(xr_in[1], 16 * (T // 2))
                dve.wait_ge(stored[1], 16 * (T // 2 - 1))
                dve.scalar_tensor_tensor(ot[1][:, H * lo:H * hi], ps[:, LAST_BANKS[lo], H * (lo % 2):H * (lo % 2 + hi - lo)],
                                         col(S_O), xr[1][:, H * lo:H * hi], ALU.mult, ALU.add).then_inc(o_sb, 1)

        @block.tensor
        def _(pe):
            def keep_clock(n, bank=6):
                for k in range(n):
                    pe.matmul(ps[:, bank, 0:P], ident[:, :], ident[:, :], start=k == 0, stop=k == n - 1)

            pe.wait_ge(const_ok, 5)
            keep_clock(WARM[0])

            def transpose_x(t):
                pe.wait_ge(x_in[t], 16)
                if t >= 1:
                    pe.wait_ge(xT_sb, t)
                for c in range(HC):
                    for q in range(Q):
                        ins = pe.transpose(ps[:, c, P * q:P * (q + 1)], xs[t][:, H * q + P * c:H * q + P * (c + 1)], ident[:, :])
                ins.then_inc(xT_ps, 1)

            def project_down(t):
                pe.wait_ge(w_in[t], 48)
                pe.wait_ge(xT_sb, t + 1)
                if t >= 1:
                    pe.wait_ge(z_sb, t)
                for c in range(HC):
                    ins = pe.matmul(ps[:, 2, :], wd[t][:, K * c:K * (c + 1)], xT[t % 2][:, S * c:S * (c + 1)],
                                    start=c == 0, stop=c == HC - 1)
                ins.then_inc(z_ps, 1)

            def project_up(t):
                pe.wait_ge(z_sb, t + 1)
                if t >= 1:
                    pe.wait_ge(y_sb, t)
                for q in range(Q):
                    ins = pe.matmul(ps[:, 3 + q // 2, H * (q % 2):H * (q % 2 + 1)], zT[t % 2][:, P * q:P * (q + 1)],
                                    wu[t], start=True, stop=True)
                    if q == Q - 1 or t == T - 1 and q == Q // 2 - 1:
                        ins.then_inc(y_ps, 1)

            def transpose_y(t):
                pe.wait_ge(yn_ok, t + 1)
                pe.wait_ge(yn2_ok, t + 1)
                if t >= 1:
                    pe.wait_ge(c_sb, HC * t)
                for c in range(HC):
                    for q in range(Q):
                        ins = pe.transpose(ps[:, 5 + c, P * q:P * (q + 1)], yn[t % 2][:, H * q + P * c:H * q + P * (c + 1)], ident[:, :])
                ins.then_inc(c_ps, 1)

            transpose_x(0)
            pe.wait_ge(prow_in, 48)
            pe.wait_ge(hot_ok, 1)
            for n in range(NPC):
                ins = pe.matmul(ps[:, 7, T * n:T * (n + 1)], prows[:, P * n:P * (n + 1)], hot[:, :], start=True, stop=True)
            ins.then_inc(pcol_ps, 1)
            for t in range(T):
                project_down(t)
                if t >= 2:
                    transpose_y(t - 2)
                if t + 1 < T:
                    transpose_x(t + 1)
                project_up(t)
            transpose_y(T - 2)

            def turn_weight(m, lo, hi, bank):
                pe.wait_ge(wdeq_ok, m + 1)
                for n in range(lo, hi):
                    if m < 2:
                        c, j = n // IC, n % IC
                        src = wdeq[m][:, H * j + P * c:H * j + P * (c + 1)]
                    else:
                        j, c = n // HC, n % HC
                        src = wdeq[m][:, I * c + P * j:I * c + P * (j + 1)]
                    ins = pe.transpose(ps[:, bank + (n - lo) // 4, P * ((n - lo) % 4):P * ((n - lo) % 4 + 1)], src, ident[:, :])
                return ins

            turn_weight(0, 0, IC * HC, 0).then_inc(wT_ps, 1)
            keep_clock(WARM[1], bank=7)
            transpose_y(T - 1)
            keep_clock(WARM[2], bank=7)

            rounds = [0]

            def spread_max(n):
                rounds[0] += 1
                pe.wait_ge(max_ok, rounds[0])
                for k in range(n):
                    ins = pe.transpose(ps[0:1, 7, P * k:P * (k + 1)], pm[:, k:k + 1], ident[:, :])
                ins.then_inc(maxT_ps, 1)
                pe.wait_ge(max_row, rounds[0])
                pe.matmul(ps[:, 7, 256:256 + n], ones[:, :], row[:, 0:n], start=True, stop=True).then_inc(max_bc, 1)

            spread_max(1)
            keep_clock(WARM[3])
            pe.wait_ge(pair_sb, 3)

            def project(wT, position, counted, pairs=range(NPAIR), by_chunks=False):
                for q in pairs:
                    pe.wait_ge(pair_sb, NPAIR * counted + q + 1)
                    for j in (2 * q, 2 * q + 1):
                        for c in range(HC):
                            if by_chunks and j == 0:
                                pe.wait_ge(cq_ok, c + 1)
                            ins = pe.matmul(ps[:, j, :], wT[:, I * c + P * j:I * c + P * (j + 1)],
                                            ubuf[:, bass.ds(TE * position + S * c, S)], start=c == 0, stop=c == HC - 1)
                    ins.then_inc(pair_ps, 1)

            project(wgT, 0, 0, by_chunks=True)
            with pe.Fori(1, T - NTURN) as t:
                pe.wait_ge(cq_ok, t + HC)
                project(wgT, t, t)
            copied = 0
            for r in range(NTURN):
                if r:
                    pe.wait_ge(wT_sb, copied)
                for m, _, lo, hi, bank in turns[r]:
                    ins = turn_weight(m, lo, hi, bank)
                    copied += 1
                ins.then_inc(wT_ps, 1)
                pe.wait_ge(cq_ok, T - NTURN + r + HC)
                project(wgT, T - NTURN + r, T - NTURN + r)
            pe.wait_ge(wT_sb, copied)
            project(wuT, KEEP, T, range(1))
            spread_max(1)
            project(wuT, KEEP, T, range(1, NPAIR))
            with pe.Fori(1, KEEP) as n:
                project(wuT, KEEP + n, T + n)
            at_h, some = divmod(SPREAD_H_AT - NPAIR * KEEP, NPAIR)
            with pe.Fori(0, at_h) as n:
                project(wuT, n, T + KEEP + n)
            project(wuT, at_h, T + KEEP + at_h, range(some))
            spread_max(1)
            project(wuT, at_h, T + KEEP + at_h, range(some, NPAIR))
            with pe.Fori(at_h + 1, KEEP) as n:
                project(wuT, n, T + KEEP + n)
            spread_max(1)
            pe.wait_ge(omax_ok, T)
            keep_clock(WARM[4])
            spread_max(1)
            keep_clock(WARM[5])

            def project_out(k, s, banks):
                for q in range(Q):
                    pe.wait_ge(oq32_ok, 2 * Q * k + Q * s + q + 1)
                    for j in range(IC):
                        ins = pe.matmul(ps[:, banks[q], H * (q % 2):H * (q % 2 + 1)],
                                        oq32[s][:, S * j + P * q:S * j + P * (q + 1)],
                                        wdT[:, H * j:H * (j + 1)], start=j == 0, stop=j == IC - 1)
                    ins.then_inc(o_ps, 1)

            pe.wait_ge(pair_sb, 3 + 2 * T * NPAIR)
            banks = [[2 * s + q // 2 for q in range(Q)] for s in range(2)]
            for s in range(2):
                project_out(0, s, banks[s])
            with pe.Fori(1, T // 2 - 1) as k:
                for s in range(2):
                    pe.wait_ge(o_sb, 2 * k + s - 1)
                    project_out(k, s, banks[s])
            pe.wait_ge(o_sb, T - 3)
            project_out(T // 2 - 1, 0, banks[0])
            pe.wait_ge(o_sb, T - 2)
            project_out(T // 2 - 1, 1, LAST_BANKS)


_INS = ["x", "itok_B_0_6", "L0_cond_down_w", "L0_cond_down_b", "L0_cond_up_w", "L0_cond_up_b", "L0_cond_ln_g",
        "L0_cond_ln_b", "L0_ffn_w_gate", "L0_ffn_w_up", "L0_ffn_w_down"]


def kernel(**inputs):
    import numpy as np
    import concourse.bacc as bacc
    from concourse import mybir as mb
    from concourse.bass_utils import run_bass_kernel_spmd

    nc = bacc.Bacc("TRN2", target_bir_lowering=False, num_devices=1)
    arrays, args = {}, []
    for name in _INS:
        a = np.ascontiguousarray(inputs[name])
        arrays[f"in_{name}"] = a
        args.append(nc.dram_tensor(f"in_{name}", a.shape, mb.dt.from_np(a.dtype), kind="ExternalInput").ap())
    shape = inputs["x"].shape
    args.append(nc.dram_tensor("out_0", shape, mb.dt.float32, kind="ExternalOutput").ap())
    adaln_ffn_kernel(nc, *args)
    r = run_bass_kernel_spmd(nc, [arrays], core_ids=[0])
    return r.results[0]["out_0"]
```
